# Optimizing a Trainium2 kernel written in Bass

```python
import numpy as np
import jax
import jax.numpy as jnp

def _softmax(x, axis=-1):
    return jax.nn.softmax(x, axis=axis)
def _gelu(x):
    return jax.nn.gelu(x, approximate=True)
def _silu(x):
    return jax.nn.silu(x)
def _sigmoid(x):
    return jax.nn.sigmoid(x)
def _layernorm(x, axis=-1, eps=1e-5):
    m = jnp.mean(x, axis=axis, keepdims=True)
    v = jnp.var(x, axis=axis, keepdims=True)
    return (x - m) / jnp.sqrt(v + eps)
def _scatter_add(tgt, idx, src, axis=0):
    return tgt.at[idx].add(src)
def _segment_sum(src, seg, n):
    return jax.ops.segment_sum(src, seg, n)

kernel_name = 'mk_conv_preact_d2_conv_nchw8_eee07d'

def setup_inputs(seed: int = 0):
    np.random.seed(seed)
    _w = jnp.asarray
    def _rec_inputs():
        import jax
        import jax.numpy as jnp
        _gk = jax.random.key(seed)
        x = 0.5003 + 0.5 * jax.random.normal(jax.random.fold_in(_gk, 1), (32, 8, 256, 256), jnp.float32)
        return x
    x = _rec_inputs()
    def _L0_conv_setup():
        import jax, jax.numpy as jnp
        import numpy as np
        N_BITS = 8
        HIDDEN = 32
        CTX = 9 * N_BITS - 1
        key = jax.random.key(seed)
        k_z, k_w1, k_b1, k_w2, k_b2 = jax.random.split(key, 5)
        B, k, H, W = (32, N_BITS, 256, 256)
        z = (jax.random.uniform(k_z, (B, k, H, W)) < 0.5).astype(jnp.float32)
        s1 = 1.0 / np.sqrt(CTX)
        s2 = 1.0 / np.sqrt(HIDDEN)
        W1 = jax.random.uniform(k_w1, (CTX, HIDDEN), minval=-s1, maxval=s1, dtype=jnp.float32)
        b1 = jax.random.uniform(k_b1, (HIDDEN,), minval=-s1, maxval=s1, dtype=jnp.float32)
        W2 = jax.random.uniform(k_w2, (HIDDEN, N_BITS), minval=-s2, maxval=s2, dtype=jnp.float32)
        b2 = jax.random.uniform(k_b2, (N_BITS,), minval=-s2, maxval=s2, dtype=jnp.float32)
        return {'z': z, 'W1': W1, 'b1': b1, 'W2': W2, 'b2': b2}
    _L0_conv_all = _L0_conv_setup()
    _L0_conv_in = {k: v for k, v in _L0_conv_all.items() if k in ('W1', 'b1', 'W2', 'b2', )}
    del _L0_conv_all

    def _L1_conv_setup():
        import jax, jax.numpy as jnp
        import numpy as np
        G = 4
        SC = 2
        WID = 10
        M1 = 12
        M2 = 12
        B = 8
        H = 256
        W = 256

        def _gconv1x1(x, w, b):
            Bb, _, Hh, Ww = x.shape
            xg = x.reshape(Bb, G, -1, Hh, Ww)
            y = jnp.einsum('bgihw,goi->bgohw', xg, w).reshape(Bb, -1, Hh, Ww)
            return y + b[None, :, None, None]

        def _gswish(x, beta):
            Bb, C, Hh, Ww = x.shape
            xg = x.reshape(Bb, G, -1, Hh, Ww)
            sp = jax.nn.softplus(beta)[None, :, None, None, None]
            return (xg * jax.nn.sigmoid(xg * sp) / 1.1).reshape(Bb, C, Hh, Ww)

        def _spectral_conv(x, w1, w2):
            Bb, _, Hh, Ww = x.shape
            Wf = Ww // 2 + 1
            xf = jnp.fft.rfft2(x).reshape(Bb, G, WID, Hh, Wf)
            w1c = w1[..., 0] + 1j * w1[..., 1]
            w2c = w2[..., 0] + 1j * w2[..., 1]
            lo = jnp.einsum('bgixy,gioxy->bgoxy', xf[:, :, :, :M1, :M2], w1c)
            hi = jnp.einsum('bgixy,gioxy->bgoxy', xf[:, :, :, Hh - M1:, :M2], w2c)
            out_ft = jnp.zeros((Bb, G, WID, Hh, Wf), jnp.complex64)
            out_ft = out_ft.at[:, :, :, :M1, :M2].set(lo)
            out_ft = out_ft.at[:, :, :, Hh - M1:, :M2].set(hi)
            return jnp.fft.irfft2(out_ft.reshape(Bb, G * WID, Hh, Wf), s=(Hh, Ww))
        key = jax.random.key(seed)
        ks = jax.random.split(key, 12)
        scale = 1.0 / (WID * WID)
        x = jax.random.normal(ks[0], (B, G * SC, H, W), jnp.float32)
        fc0_w = jax.random.normal(ks[1], (G, WID, SC + 2), jnp.float32) * 0.1
        fc0_b = jax.random.normal(ks[2], (G * WID,), jnp.float32) * 0.01
        w_w = jax.random.normal(ks[3], (4, G, WID, WID), jnp.float32) * 0.1
        w_b = jax.random.normal(ks[4], (4, G * WID), jnp.float32) * 0.01
        sp_w1 = scale * jax.random.uniform(ks[5], (4, G, WID, WID, M1, M2, 2), jnp.float32)
        sp_w2 = scale * jax.random.uniform(ks[6], (4, G, WID, WID, M1, M2, 2), jnp.float32)
        betas = jnp.full((4, G), 0.5, jnp.float32)
        fc1_w = jax.random.normal(ks[7], (G, 128, WID), jnp.float32) * 0.05
        fc1_b = jax.random.normal(ks[8], (G * 128,), jnp.float32) * 0.01
        fc2_w = jax.random.normal(ks[9], (G, SC, 128), jnp.float32) * 0.05
        fc2_b = jax.random.normal(ks[10], (G * SC,), jnp.float32) * 0.01
        return {'x': x, 'fc0_w': fc0_w, 'fc0_b': fc0_b, 'w_w': w_w, 'w_b': w_b, 'sp_w1': sp_w1, 'sp_w2': sp_w2, 'betas': betas, 'fc1_w': fc1_w, 'fc1_b': fc1_b, 'fc2_w': fc2_w, 'fc2_b': fc2_b}
    _L1_conv_all = _L1_conv_setup()
    _L1_conv_in = {k: v for k, v in _L1_conv_all.items() if k in ('fc0_w', 'fc0_b', 'w_w', 'w_b', 'sp_w1', 'sp_w2', 'betas', 'fc1_w', 'fc1_b', 'fc2_w', 'fc2_b', )}
    del _L1_conv_all

    return {
        "x": x,
        "L0_conv_W1": _L0_conv_in["W1"],
        "L0_conv_b1": _L0_conv_in["b1"],
        "L0_conv_W2": _L0_conv_in["W2"],
        "L0_conv_b2": _L0_conv_in["b2"],
        "L1_conv_fc0_w": _L1_conv_in["fc0_w"],
        "L1_conv_fc0_b": _L1_conv_in["fc0_b"],
        "L1_conv_w_w": _L1_conv_in["w_w"],
        "L1_conv_w_b": _L1_conv_in["w_b"],
        "L1_conv_sp_w1": _L1_conv_in["sp_w1"],
        "L1_conv_sp_w2": _L1_conv_in["sp_w2"],
        "L1_conv_betas": _L1_conv_in["betas"],
        "L1_conv_fc1_w": _L1_conv_in["fc1_w"],
        "L1_conv_fc1_b": _L1_conv_in["fc1_b"],
        "L1_conv_fc2_w": _L1_conv_in["fc2_w"],
        "L1_conv_fc2_b": _L1_conv_in["fc2_b"],
    }

def reference(x, L0_conv_W1, L0_conv_b1, L0_conv_W2, L0_conv_b2, L1_conv_fc0_w, L1_conv_fc0_b, L1_conv_w_w, L1_conv_w_b, L1_conv_sp_w1, L1_conv_sp_w2, L1_conv_betas, L1_conv_fc1_w, L1_conv_fc1_b, L1_conv_fc2_w, L1_conv_fc2_b):
    import jax
    import jax.numpy as jnp
    def _L0_conv_ref(z, W1, b1, W2, b2):
        import jax, jax.numpy as jnp
        import numpy as np
        N_BITS = 8
        HIDDEN = 32
        CTX = 9 * N_BITS - 1
        B, k, H, W = z.shape
        zp = jnp.pad(z, ((0, 0), (0, 0), (1, 1), (1, 1)))
        patches = jnp.stack([zp[:, :, di:di + H, dj:dj + W] for di in range(3) for dj in range(3)], axis=2)
        mask = jnp.ones((9,), z.dtype).at[4].set(0.0)
        patches = patches * mask[None, None, :, None, None]
        feat = patches.reshape(B, k * 9, H, W).transpose(0, 2, 3, 1)[..., :9 * k - 1]
        h = jax.nn.relu(jnp.einsum('bhwc,cd->bhwd', feat, W1) + b1)
        logits = jnp.einsum('bhwd,dn->bhwn', h, W2) + b2
        return logits.transpose(0, 3, 1, 2)

    def _L1_conv_ref(x, fc0_w, fc0_b, w_w, w_b, sp_w1, sp_w2, betas, fc1_w, fc1_b, fc2_w, fc2_b):
        import jax, jax.numpy as jnp
        import numpy as np
        G = 4
        SC = 2
        WID = 10
        M1 = 12
        M2 = 12
        B = 8
        H = 256
        W = 256

        def _gconv1x1(x, w, b):
            Bb, _, Hh, Ww = x.shape
            xg = x.reshape(Bb, G, -1, Hh, Ww)
            y = jnp.einsum('bgihw,goi->bgohw', xg, w).reshape(Bb, -1, Hh, Ww)
            return y + b[None, :, None, None]

        def _gswish(x, beta):
            Bb, C, Hh, Ww = x.shape
            xg = x.reshape(Bb, G, -1, Hh, Ww)
            sp = jax.nn.softplus(beta)[None, :, None, None, None]
            return (xg * jax.nn.sigmoid(xg * sp) / 1.1).reshape(Bb, C, Hh, Ww)

        def _spectral_conv(x, w1, w2):
            Bb, _, Hh, Ww = x.shape
            Wf = Ww // 2 + 1
            xf = jnp.fft.rfft2(x).reshape(Bb, G, WID, Hh, Wf)
            w1c = w1[..., 0] + 1j * w1[..., 1]
            w2c = w2[..., 0] + 1j * w2[..., 1]
            lo = jnp.einsum('bgixy,gioxy->bgoxy', xf[:, :, :, :M1, :M2], w1c)
            hi = jnp.einsum('bgixy,gioxy->bgoxy', xf[:, :, :, Hh - M1:, :M2], w2c)
            out_ft = jnp.zeros((Bb, G, WID, Hh, Wf), jnp.complex64)
            out_ft = out_ft.at[:, :, :, :M1, :M2].set(lo)
            out_ft = out_ft.at[:, :, :, Hh - M1:, :M2].set(hi)
            return jnp.fft.irfft2(out_ft.reshape(Bb, G * WID, Hh, Wf), s=(Hh, Ww))
        Bb, _, Hh, Ww = x.shape
        gridx = jnp.broadcast_to(jnp.linspace(0.0, 1.0, Hh)[:, None], (Hh, Ww))
        gridy = jnp.broadcast_to(jnp.linspace(0.0, 1.0, Ww)[None, :], (Hh, Ww))
        grid = jnp.stack([gridx, gridy], axis=0)
        xg = x.reshape(Bb, G, SC, Hh, Ww)
        gridb = jnp.broadcast_to(grid[None, None], (Bb, G, 2, Hh, Ww))
        h = jnp.concatenate([xg, gridb], axis=2).reshape(Bb, G * (SC + 2), Hh, Ww)
        h = _gconv1x1(h, fc0_w, fc0_b)
        for i in range(4):
            h1 = _spectral_conv(h, sp_w1[i], sp_w2[i])
            h2 = _gconv1x1(h, w_w[i], w_b[i])
            h = h1 + h2
            if i < 3:
                h = _gswish(h, betas[i])
        h = _gswish(_gconv1x1(h, fc1_w, fc1_b), betas[3])
        return _gconv1x1(h, fc2_w, fc2_b)

    def _gn(v, G=4, eps=1e-5):
        B_, C_, H_, W_ = v.shape
        g = v.reshape(B_, G, C_ // G, H_, W_)
        m = jnp.mean(g, axis=(2, 3, 4), keepdims=True)
        s = jnp.var(g, axis=(2, 3, 4), keepdims=True)
        return ((g - m) / jnp.sqrt(s + eps)).reshape(v.shape)

    def _ln_c(v, eps=1e-6):
        m = jnp.mean(v, axis=1, keepdims=True)
        s = jnp.var(v, axis=1, keepdims=True)
        return (v - m) / jnp.sqrt(s + eps)

    def _ln_t(v, eps=1e-5):
        m = jnp.mean(v, axis=-1, keepdims=True)
        s = jnp.var(v, axis=-1, keepdims=True)
        return (v - m) / jnp.sqrt(s + eps)

    def _to_tokens(v):
        B_, C_, H_, W_ = v.shape
        return v.reshape(B_, C_, H_ * W_).transpose(0, 2, 1)
    def _from_tokens(t, like):
        B_, C_, H_, W_ = like.shape
        return t.transpose(0, 2, 1).reshape(B_, C_, H_, W_)

    x = x + _L0_conv_ref(_gn(x), L0_conv_W1, L0_conv_b1, L0_conv_W2, L0_conv_b2)
    x = x + _L1_conv_ref(_gn(x), L1_conv_fc0_w, L1_conv_fc0_b, L1_conv_w_w, L1_conv_w_b, L1_conv_sp_w1, L1_conv_sp_w2, L1_conv_betas, L1_conv_fc1_w, L1_conv_fc1_b, L1_conv_fc2_w, L1_conv_fc2_b)
    return x


_drawn_inputs = setup_inputs


def setup_inputs(seed=0):
    import zlib

    import numpy as np

    out = dict(_drawn_inputs(seed))
    spreads = {'L1_conv_betas': (0.5, 0.6)}
    factors = {'L1_conv_fc0_w': 8.0,
     'L1_conv_fc0_b': 8.0,
     'L1_conv_w_w': 8.0,
     'L1_conv_w_b': 8.0,
     'L1_conv_sp_w1': 8.0,
     'L1_conv_sp_w2': 46.034,
     'L1_conv_fc1_w': 8.0,
     'L1_conv_fc1_b': 62.758,
     'L1_conv_fc2_w': 8.0,
     'L1_conv_fc2_b': 200.0}
    for name, (base, spread) in spreads.items():
        noise = np.random.default_rng([zlib.crc32(name.encode()), seed]).standard_normal(out[name].shape)
        drawn = base * np.exp(spread * noise) if base else spread * noise
        out[name] = jnp.asarray(drawn.astype(out[name].dtype))
    for name, factor in factors.items():
        out[name] = (out[name] * factor).astype(out[name].dtype)
    return out
```

```python
from contextlib import ExitStack

import numpy as np
import concourse.bass as bass
from concourse import mybir
from concourse.alu_op_type import AluOpType as ALU

F32 = mybir.dt.float32
F32R = mybir.dt.float32r
ACT = mybir.ActivationFunctionType
AXIS = mybir.AxisListType

C, H, W = 8, 256, 256
HID = 32
G, SC, WID = 4, 2, 10
CH = G * WID
LAYERS = 4
KX, KY = 24, 12
FF = 128
PIX = H * W
ROW2 = 2 * W
PAD = W + 2
NBLK, BROWS, BSTEP = 3, 88, 84
PAIRS = BROWS // 2
BPIX = BROWS * W
CHUNKS = 8
XGRP = 11
FCH = 4
NFC = PAIRS // FCH
EPS = 1e-5
SHRINK = 1.1



def fourier_tables():
    kx = np.concatenate([np.arange(KX // 2), np.arange(-KX // 2, 0)])
    ky = np.arange(KY)
    row = 2 * np.pi / H * np.outer(np.arange(H), kx)
    col = 2 * np.pi / W * np.outer(np.arange(W), ky)
    fwd_row = np.concatenate([np.cos(row), -np.sin(row)], 1).reshape(2, 128, 2 * KX).transpose(1, 0, 2)
    c, s = np.cos(col), np.sin(col)
    from_re = np.concatenate([np.stack([c, s], -1).reshape(W, -1), np.stack([-s, c], -1).reshape(W, -1)], 1)
    from_im = np.concatenate([np.stack([s, -c], -1).reshape(W, -1), np.stack([c, s], -1).reshape(W, -1)], 1)
    fwd_col = np.stack([from_re, from_im], 1).reshape(2, 128, 2, 4 * KY).transpose(1, 0, 2, 3)
    inv_row = np.zeros((128, 2, H))
    for g in range(G):
        inv_row[32 * g:32 * g + KX, 0] = np.cos(row).T
        inv_row[32 * g:32 * g + KX, 1] = np.sin(row).T
    weight = np.where(ky == 0, 1.0, 2.0)[:, None] / (H * W)
    inv_col = np.zeros((32 * NBLK, W))
    for k in range(NBLK):
        inv_col[32 * k:32 * k + KY] = weight * c.T
        inv_col[32 * k + KY:32 * k + 2 * KY] = -weight * s.T
    f = lambda a: np.ascontiguousarray(a, np.float32)
    return f(fwd_row), f(fwd_col), f(inv_row), f(inv_col)


def grid_rows():
    gx = np.linspace(0.0, 1.0, H, dtype=np.float32)
    gy = np.linspace(0.0, 1.0, W, dtype=np.float32)
    rows = [np.repeat(gx[BSTEP * k:BSTEP * k + BROWS], W) for k in range(NBLK)]
    return np.stack([*rows, np.tile(gy, BROWS)]).astype(np.float32)


def group_mean():
    g = (np.arange(128) % C) // SC
    return np.where(g[:, None] == g[None], G / 128.0, 0.0).astype(np.float32)


def split_signs():
    s = np.zeros((3 * CH, 3), np.float32)
    s[CH:2 * CH, 0] = 1.0
    s[2 * CH:, 1] = -1.0
    s[:CH, 2] = -1.0
    s[CH:, 2] = 1.0
    return s


def program(nc, nb, x, conv1_w, conv1_b, conv2_w, conv2_b, lift_w, lift_b, mix_w, mix_b, spec_w, betas, fc1_w, fc1_b,
          fc2_w, fc2_b, fwd_row, fwd_col, inv_row, inv_col, grid, gmean, signs, out):
    with ExitStack() as ctx:
        def sb(name, shape, dt=F32):
            return ctx.enter_context(nc.sbuf_tensor(name, shape, dt))

        def sem(name):
            return ctx.enter_context(nc.semaphore(name))

        zpad = nc.dram_tensor("zpad", [C, H + 2, PAD], F32, kind="Internal")
        x1_d = nc.dram_tensor("x1_d", [C, H, W], F32, kind="Internal")
        x1n_d = nc.dram_tensor("x1n_d", [C, H, W], F32, kind="Internal")
        h_d = nc.dram_tensor("h_d", [CH, H, W], F32, kind="Internal")

        hmem = sb("hmem", [128, BPIX])
        h = hmem[0:NBLK * CH, :]
        xt = hmem[:, 0:4096]
        x1t = hmem[:, 4096:8192]
        zt = hmem[:, 8192:12288]
        col = [hmem[:, 12288 + 4096 * n:16384 + 4096 * n] for n in range(2)]
        hid = [hmem[:, 20480 + 512 * n:20992 + 512 * n] for n in range(2)]
        arena = sb("arena", [128, 6144])
        xc = arena[0:28, 0:XGRP * ROW2]
        himg = [arena[:, 2560 * n:2560 * n + 2560] for n in range(2)]
        prod = arena[:, 0:2400]
        s1 = sb("s1", [128, 2 * 2 * WID * 128])
        s1v = s1[:, :].rearrange("p (h r c m) -> p h r c m", h=2, r=2, c=WID)
        z3 = [arena[0:3 * CH, 2048 * n:2048 * n + 2048] for n in range(3)]
        fsb = arena[:, 2400:2880].rearrange("p (c f) -> p c f", c=WID)
        act = [s1[:, 1024 * n:1024 * n + 1024] for n in range(2)]
        high = s1[0:3 * CH, 2048:3072]
        xr = s1[0:96, 3072:3584]
        ob = s1[0:96, 3584:4096]
        split = [sb(f"split{n}", [3 * CH, 1024], F32R) for n in range(2)]
        gst = sb("gst", [32 * NBLK, BROWS * NBLK * CH])
        gstv = gst[:, :].rearrange("p (y c) -> p y c", c=NBLK * CH)
        wspec = sb("wspec", [128, WID * WID * 2 * KY])

        c1w = sb("c1w", [128, 64]); c1b = sb("c1b", [128, 1]); c2w = sb("c2w", [128, 32]); c2b = sb("c2b", [128, 1])
        liftw = sb("liftw", [28, NBLK * CH]); hb = sb("hb", [NBLK * CH, 1 + LAYERS])
        mixw = sb("mixw", [NBLK * CH, LAYERS, NBLK * CH])
        mixl = sb("mixl", [NBLK * CH, NBLK * CH])
        layb = sb("layb", [NBLK * CH, 2])
        power = sb("power", [128, 1])
        idle = sb("idle", [128, 1])
        beta = sb("beta", [128, 12]); sp = sb("sp", [128, 12]); spt = sb("spt", [128, 12]); rsp = sb("rsp", [128, 12])
        fscale = sb("fscale", [128, LAYERS])
        f1w = sb("f1w", [3 * CH, G * FF], F32R); f1b = sb("f1b", [128, G])
        f2w = sb("f2w", [128, G, FCH, 32]); f2b = sb("f2b", [128, 1])
        fwdr = sb("fwdr", [128, 2, 2 * KX]); fwdc = sb("fwdc", [128, 2, 2, 4 * KY])
        invr = sb("invr", [128, 2, H]); invc = sb("invc", [32 * NBLK, W])
        gm = sb("gm", [128, 128]); sg = sb("sg", [3 * CH, 3])
        stats = sb("stats", [128, CHUNKS, 6]); mv = sb("mv", [128, 8])
        ot = sb("ot", [128, 2, 12, 32])

        PS = ctx.enter_context(nc.psum_tensor("PS", [128, 8, 512], F32))
        gnps = PS[:, 7, :]

        s_w = sem("weights_loaded"); s_set = sem("setup_vector"); s_sact = sem("setup_scalar")
        s_zero = sem("border_zeroed")
        s_x = sem("x_loaded"); s_stin = sem("stats_in"); s_stps = sem("stats_summed"); s_var = sem("variance")
        s_rstd = sem("rstd"); s_z = sem("z_ready"); s_zst = sem("z_stored")
        s_col = [sem("col0_loaded"), sem("col1_loaded")]
        s_mm1 = sem("conv1_done"); s_relu = sem("relu_done"); s_mm2 = sem("conv2_done"); s_x1 = sem("x1_chunk")
        s_x1st = sem("x1_stored"); s_xc = sem("lift_input")
        s_row = sem("rows_summed"); s_hrow = sem("rows_ready"); s_hst = sem("h_stored")
        s_himg = [sem("image0_loaded"), sem("image1_loaded")]; s_wsp = sem("spectral_weights")
        s_st1 = sem("row_transform"); s_s1ev = sem("row_transform_kept"); s_st2 = sem("column_transform")
        s_ot = sem("modes_mixed"); s_g = sem("inverse_rows"); s_gA = sem("inverse_rows_kept_scalar")
        s_gD = sem("inverse_rows_kept_vector")
        s_T = [sem(f"z3_{k}_loaded") for k in range(3)]
        s_tm = sem("operand_split"); s_fc1 = sem("fc1_done"); s_silu = sem("silu_done"); s_fc2 = sem("fc2_done")
        s_xr = sem("residual_loaded"); s_fo = sem("result_ready"); s_out = sem("result_stored")

        HEAD, HEAD_MM1, HEAD_TM = 8, 4, 6
        OUT_PER = NFC * NBLK * 16
        consts = [(c1w[:, :], conv1_w), (c1b[:, :], conv1_b), (c2w[:, :], conv2_w), (c2b[:, :], conv2_b),
                  (liftw[:, :], lift_w), (hb[:, 0:1], lift_b), (hb[:, 1:1 + LAYERS], mix_b), (mixw[:, :, :], mix_w),
                  (beta[:, :], betas), (arena[0:3 * CH, 0:G * FF], fc1_w), (f1b[:, :], fc1_b), (f2w[:, :, :, :], fc2_w),
                  (f2b[:, :], fc2_b), (fwdr[:, :, :], fwd_row), (fwdc[:, :, :, :], fwd_col), (invr[:, :, :], inv_row),
                  (invc[:, :], inv_col), (gm[:, :], gmean), (sg[:, :], signs)]
        raw1 = arena[0:3 * CH, 0:G * FF]
        half1 = arena[0:3 * CH, G * FF:2 * G * FF]

        SETUP_V = 4

        def inverse_parts(n):
            parts = []
            for slot in (n, n + 2):
                for k in range(NBLK):
                    y = BSTEP * k
                    src = PS[32 * slot:32 * slot + 2 * KY, 0:4, :].rearrange("p g (s y) -> p g s y", s=2)
                    dst = gstv[32 * k:32 * k + 2 * KY, :, CH * k:CH * k + CH].rearrange("p y (g o) -> p g o y", g=G)
                    parts.append((dst[:, :, slot:slot + 5:4, :], src[:, :, :, y:y + BROWS]))
                    if slot < 2:
                        parts.append((dst[:, :, 8 + slot, :], PS[32 * slot:32 * slot + 2 * KY, 4:8, y:y + BROWS]))
            return parts

        GP = [len(inverse_parts(n)) for n in range(2)]

        block = ctx.enter_context(nc.Block())

        def pieces(dram, img, m):
            return [bass.AP(dram, img + half * 128 * W + m * ROW2, [[PIX, C], [16 * W, CHUNKS], [1, ROW2]])
                    for half in range(2)]

        @block.sync
        def _(sp_):
            for dst, src in consts:
                sp_.dma_start(dst, src).then_inc(s_w, 16)
            sp_.wait_ge(s_set, 1)
            sp_.dma_start(bass.AP(zpad, 0, [[5547, 96], [1, 5547]]), gst[:, 0:5547]).then_inc(s_zero, 16)
            sp_.wait_ge(s_zero, 16)
            with sp_.Fori(0, nb) as i:
                sp_.wait_ge(s_out, i * OUT_PER)
                for m in range(8):
                    for half, src in enumerate(pieces(x, i * (C * PIX), m)):
                        p = 16 * m + 8 * half
                        sp_.dma_start(xt[p:p + 8, :].rearrange("p (a b) -> p a b", a=CHUNKS), src).then_inc(s_x, 16)
                sp_.wait_ge(s_z, i * 2 + 1)
                for m in range(8):
                    for half in range(2):
                        p = 16 * m + 8 * half
                        for r in range(2):
                            y = 128 * half + 2 * m + r
                            dst = bass.AP(zpad, (y + 1) * PAD + 1, [[(H + 2) * PAD, C], [16 * PAD, CHUNKS], [1, W]])
                            src = zt[p:p + 8, :].rearrange("p (a b) -> p a b", a=CHUNKS)[:, :, r * W:r * W + W]
                            sp_.dma_start(dst, src).then_inc(s_zst, 16)
                with sp_.Fori(0, CHUNKS // 2) as j:
                    for par in range(2):
                        if par == 0:
                            sp_.wait_ge(s_zst, (i + 1) * 512)
                        sp_.wait_ge(s_mm1, i * 32 + (j * 2 + par) * 4)
                        for half in range(2):
                            for dy in range(3):
                                for dx in (0, 2) if dy == 1 else (0, 1, 2):
                                    tap = 3 * dy + dx - (3 * dy + dx > 4)
                                    p = 64 * half + tap * C
                                    at = (j * 2 + par) * (16 * PAD) + (128 * half + dy) * PAD + dx
                                    sp_.dma_start(
                                        col[par][p:p + 8, :].rearrange("p (a b) -> p a b", b=W),
                                        bass.AP(zpad, at, [[(H + 2) * PAD, C], [PAD, 16], [1, W]]),
                                    ).then_inc(s_col[par], 16)
                sp_.wait_ge(s_x1, i * 8 + 8)
                for m in range(8):
                    for half, dst in enumerate(pieces(x1_d, 0, m)):
                        p = 16 * m + 8 * half
                        sp_.dma_start(dst, x1t[p:p + 8, :].rearrange("p (a b) -> p a b", a=CHUNKS)).then_inc(s_x1st, 16)
                sp_.wait_ge(s_z, i * 2 + 2)
                for m in range(8):
                    for half, dst in enumerate(pieces(x1n_d, 0, m)):
                        p = 16 * m + 8 * half
                        sp_.dma_start(dst, zt[p:p + 8, :].rearrange("p (a b) -> p a b", a=CHUNKS)).then_inc(s_x1st, 16)
                with sp_.Fori(0, PAIRS // XGRP) as j:
                    sp_.wait_ge(s_x1st, (i + 1) * 512)
                    sp_.wait_ge(s_row, i * 220 + j * XGRP)
                    for k in range(NBLK):
                        sp_.dma_start(xc[8 * k:8 * k + 8, :],
                                      bass.AP(x1n_d, j * (XGRP * ROW2) + k * BSTEP * W, [[PIX, C], [1, XGRP * ROW2]])
                                      ).then_inc(s_xc, 16)
                    sp_.dma_start(xc[24:28, :], grid[:, bass.ds(j * (XGRP * ROW2), XGRP * ROW2)]).then_inc(s_xc, 16)
                with sp_.Fori(0, LAYERS) as l:
                    sp_.wait_ge(s_ot, i * 4 + l)
                    sp_.dma_start(wspec[:, :], spec_w[bass.ds(l, 1), :, :].rearrange("a p n -> (a p) n")).then_inc(s_wsp, 16)
                    for q in range(PAIRS // XGRP):
                        sp_.wait_ge(s_hrow, i * 220 + l * 44 + XGRP * (q + 1))
                        for k in range(NBLK):
                            y0 = 2 * XGRP * q
                            n = min(2 * XGRP, (BSTEP if k < NBLK - 1 else BROWS) - y0)
                            sp_.dma_start(bass.AP(h_d, (BSTEP * k + y0) * W, [[PIX, CH], [1, n * W]]),
                                          hmem[CH * k:CH * k + CH, y0 * W:(y0 + n) * W]).then_inc(s_hst, 16)
                    sp_.wait_ge(s_hst, (i * 4 + l + 1) * 192)
                    for c in range(8):
                        if c >= 2:
                            sp_.wait_ge(s_st1, (i * 4 + l) * 8 + (c - 1))
                        for t in range(2):
                            sp_.dma_start(himg[c % 2].rearrange("p (t c x) -> p t c x", t=2, c=5)[:, t],
                                          bass.AP(h_d, 5 * c * PIX + t * 128 * W, [[W, 128], [PIX, 5], [1, W]])
                                          ).then_inc(s_himg[c % 2], 16)
                with sp_.Fori(0, NFC) as c:
                    sp_.wait_ge(s_hrow, i * 220 + 220)
                    for k in range(NBLK):
                        sp_.wait_ge(s_tm, i * 66 + c * 6 + (2 * k + 2))
                        for r in range(3):
                            sp_.dma_start(z3[k][CH * r:CH * r + CH, :],
                                          hmem[CH * k:CH * k + CH, bass.ds(c * (FCH * ROW2), FCH * ROW2)]
                                          ).then_inc(s_T[k], 16)
            sp_.wait_ge(s_out, nb * OUT_PER)

        @block.tensor
        def _(pe):
            pe.wait_ge(s_w, 16 * len(consts))
            pe.wait_ge(s_set, SETUP_V)
            pe.sem_inc(s_fc1, HEAD)
            pe.sem_inc(s_mm1, HEAD_MM1)
            with pe.Fori(0, nb) as i:
                def group_sums(n):
                    for r in range(2):
                        pe.wait_ge(s_stin, i * 4 + 2 * n + r + 1)
                        nc.tensor.matmul(gnps[:, r:r + 1], gm[:, :], mv[:, 3 * r:3 * r + 1],
                                         start=True, stop=True).then_inc(s_stps, 1)

                group_sums(0)
                with pe.Fori(0, CHUNKS // 2) as j:
                    for par in range(2):
                        chunk = i * 8 + j * 2 + par
                        pe.wait_ge(s_col[par], (i * 4 + j + 1) * 256)

                        def second(q):
                            pe.wait_ge(s_relu, chunk * 4 + q + 1)
                            if q == 0:
                                pe.wait_ge(s_x1, chunk)
                            mm = nc.tensor.matmul(PS[32 * q:32 * q + 32, 2, :], c2w[:, :], hid[q % 2],
                                                  start=True, stop=True, tile_position=(0, 32 * q))
                            if q == 3:
                                mm.then_inc(s_mm2, 1)

                        for q in range(4):
                            for u in range(2):
                                mm = nc.tensor.matmul(PS[64 * u:64 * u + 64, q % 2, :], c1w[:, :],
                                                      col[par][:, (2 * q + u) * ROW2:(2 * q + u + 1) * ROW2],
                                                      start=True, stop=True, tile_position=(0, 64 * u))
                            mm.then_inc(s_mm1, 1)
                            if q:
                                second(q - 1)
                        second(3)
                group_sums(1)
                with pe.Fori(0, PAIRS // XGRP) as j:
                    pe.wait_ge(s_xc, (i * 4 + j + 1) * 64)
                    for p in range(XGRP):
                        pe.wait_ge(s_hrow, i * 220 + j * XGRP + max(p - 3, 0))
                        mm = nc.tensor.matmul(PS[0:NBLK * CH, p % 4, :], liftw[:, :], xc[:, p * ROW2:(p + 1) * ROW2],
                                              start=True, stop=True).then_inc(s_row, 1)

                with pe.Fori(0, LAYERS) as l:
                    lay = i * 4 + l
                    for c in range(8):
                        pe.wait_ge(s_himg[c % 2], lay * 128 + (c // 2 + 1) * 32)
                        if c >= 2:
                            pe.wait_ge(s_s1ev, lay * 16 + 2 * (c - 1))
                        im = himg[c % 2].rearrange("p (t c x) -> p t c x", t=2, c=5)
                        for ch in range(5):
                            for xh in range(2):
                                at = (xh * 5 + ch) * 48
                                for t in range(2):
                                    mm = nc.tensor.matmul(PS[:, 4 + c % 2, at:at + 48], im[:, t, ch, 128 * xh:128 * xh + 128],
                                                          fwdr[:, t, :], start=t == 0, stop=t == 1)
                        mm.then_inc(s_st1, 1)
                    pe.wait_ge(s_s1ev, lay * 16 + 16)
                    for ch in range(WID):
                        n = 0
                        for xh in range(2):
                            for r in range(2):
                                mm = nc.tensor.matmul(PS[:, 6, ch * 48:ch * 48 + 48], s1v[:, xh, r, ch, :],
                                                      fwdc[:, xh, r, :], start=n == 0, stop=n == 3)
                                n += 1
                    mm.then_inc(s_st2, 1)
                    pe.wait_ge(s_ot, lay + 1)
                    for g in range(G):
                        for s in (2, 0, 1):
                            bank, at = (4 + g, 0) if s == 2 else (g, 256 * s)
                            for cs in range(2):
                                mm = nc.tensor.matmul(PS[:, bank, at:at + 256],
                                                      ot[32 * g:32 * g + 32, cs, 4 * s:4 * s + 4, :].rearrange("p a b -> p (a b)"),
                                                      invr[32 * g:32 * g + 32, cs, :], start=cs == 0, stop=cs == 1,
                                                      tile_position=(32 * g, 0))
                    mm.then_inc(s_g, 1)
                    pe.wait_ge(s_gA, lay * GP[0] + GP[0])
                    pe.wait_ge(s_gD, lay * GP[1] + GP[1])
                    for p in range(PAIRS):
                        if p >= 4:
                            pe.wait_ge(s_hrow, i * 220 + l * 44 + 44 + p - 3)
                        nc.tensor.matmul(PS[0:NBLK * CH, p % 4, :], mixl[:, :], h[:, p * ROW2:(p + 1) * ROW2],
                                         start=True, stop=True)
                        for r in range(2):
                            mm = nc.tensor.matmul(PS[0:NBLK * CH, p % 4, r * W:r * W + W], gstv[:, 2 * p + r, :], invc[:, :],
                                                  start=False, stop=True, skip_group_check=True)
                        mm.then_inc(s_row, 1)

                with pe.Fori(0, NFC) as c:
                    step = HEAD + (i * NFC + c) * 24

                    def fc2(s):
                        u, g = divmod(s, G)
                        k, half = divmod(u, 2)
                        pe.wait_ge(s_silu, (i * NFC + c) * 24 + s + 1)
                        if s == 0:
                            pe.wait_ge(s_fo, i * NFC + c)
                        for p in range(2):
                            mm = nc.tensor.matmul(PS[32 * k:32 * k + 32, 6, :], f2w[:, g, 2 * half + p, :],
                                                  act[s % 2][:, p * 512:p * 512 + 512],
                                                  start=g == 0 and half == 0 and p == 0, stop=g == 3 and half == 1 and p == 1,
                                                  tile_position=(0, 32 * k))
                        if s == 23:
                            mm.then_inc(s_fc2, 1)

                    for s in range(24):
                        u, g = divmod(s, G)
                        if g == 0:
                            pe.wait_ge(s_tm, i * 66 + c * 6 + (u + 1 + HEAD_TM))
                        for p in range(2):
                            mm = nc.tensor.matmul(PS[:, 2 * (s % 3) + p, :], f1w[:, g * FF:g * FF + FF],
                                                  split[u % 2][:, p * 512:p * 512 + 512], start=True, stop=True)
                        mm.then_inc(s_fc1, 1)
                        if s:
                            fc2(s - 1)
                    fc2(23)

        @block.scalar
        def _(act_):
            act_.wait_ge(s_w, 16 * len(consts))
            act_.wait_ge(s_set, 2)
            nc.scalar.activation(rsp[:, :], spt[:, :], ACT.Exp).then_inc(s_sact, 1)
            act_.wait_ge(s_set, 3)
            nc.scalar.activation(spt[:, :], sp[:, :], ACT.Ln).then_inc(s_sact, 1)
            act_.wait_ge(s_set, SETUP_V)

            def rows(lead, pass_, bias, scale, func, group=PAIRS):
                for p in range(PAIRS):
                    act_.wait_ge(s_row, lead + pass_ * 44 + p + 1)
                    bank = (p % group) % 4
                    nc.scalar.activation(h[:, p * ROW2:(p + 1) * ROW2], PS[0:NBLK * CH, bank, :], func,
                                         bias=bias, scale=scale).then_inc(s_hrow, 1)

            def transforms(lay):
                for c in range(8):
                    act_.wait_ge(s_st1, lay * 8 + (c + 1))
                    if c == 0:
                        act_.wait_ge(s_st2, lay)
                    o = 5 * (c % 2)
                    for xh in range(2):
                        src = PS[:, 4 + c % 2, xh * 240:xh * 240 + 240].rearrange("p (c r k) -> p c r k", c=5, r=2)
                        for r in range(2):
                            e = nc.scalar.activation(s1v[:, xh, r, o:o + 5, 32 * (c // 2):32 * (c // 2) + KX],
                                                     src[:, :, r, :], ACT.Identity)
                            if r:
                                e.then_inc(s_s1ev, 1)
                act_.wait_ge(s_g, lay + 1)
                for e in inverse_parts(0):
                    nc.scalar.activation(*e, ACT.Identity).then_inc(s_gA, 1)

            with act_.Fori(0, nb) as i:
                with act_.Fori(0, CHUNKS // 2) as j:
                    for n in range(8):
                        act_.wait_ge(s_mm1, i * 32 + j * 8 + (n + 1 + HEAD_MM1))
                        nc.scalar.activation(hid[n % 2], PS[:, n % 2, :], ACT.Relu, bias=c1b[:, 0:1]).then_inc(s_relu, 1)
                rows(i * 220, 0, hb[:, 0:1], 1.0, ACT.Identity, XGRP)
                with act_.Fori(0, LAYERS - 1) as l:
                    transforms(i * 4 + l)
                    rows(i * 220, l + 1, layb[:, 0:1], layb[:, 1:2], ACT.Silu)
                transforms(i * 4 + (LAYERS - 1))
                rows(i * 220, LAYERS, hb[:, LAYERS:LAYERS + 1], 1.0, ACT.Identity)
                with act_.Fori(0, NFC) as c:
                    for s in range(24):
                        g = s % G
                        act_.wait_ge(s_fc1, i * (24 * NFC) + c * 24 + (s + 1 + HEAD))
                        pair = 2 * (s % 3)
                        nc.scalar.activation(act[s % 2], PS[:, pair:pair + 2, :].rearrange("p a b -> p (a b)"), ACT.Silu,
                                             bias=f1b[:, g:g + 1], scale=sp[:, 8 + g:9 + g]).then_inc(s_silu, 1)

        @block.vector
        def _(dve):
            V = nc.vector
            dve.sem_inc(s_tm, HEAD_TM)
            V.memset(gst[:, :], 0.0)
            V.memset(s1[:, :], 0.0)
            V.memset(ot[:, :, :, :], 0.0)
            V.memset(power[:, :], -0.5)
            V.drain().then_inc(s_set, 1)
            dve.wait_ge(s_w, 16 * len(consts))
            V.tensor_scalar(sp[:, :], beta[:, :], -1.0, None, ALU.mult)
            V.drain()
            V.tensor_tensor(spt[:, :], beta[:, :], sp[:, :], ALU.min)
            V.drain().then_inc(s_set, 1)
            dve.wait_ge(s_sact, 1)
            V.tensor_scalar(sp[:, :], rsp[:, :], 1.0, None, ALU.add)
            V.drain().then_inc(s_set, 1)
            dve.wait_ge(s_sact, 2)
            V.tensor_scalar(sp[:, :], beta[:, :], 0.0, None, ALU.max)
            V.drain()
            V.tensor_tensor(sp[:, :], sp[:, :], spt[:, :], ALU.add)
            V.drain()
            V.tensor_scalar(sp[:, :], sp[:, :], 1e-20, SHRINK, ALU.max, ALU.mult)
            V.drain()
            V.reciprocal(rsp[:, :], sp[:, :])
            V.tensor_scalar(sp[:, :], sp[:, :], 1.0 / SHRINK, None, ALU.mult)
            V.drain()
            V.memset(fscale[:, 0:1], 1.0)
            V.tensor_copy(fscale[:, 1:LAYERS], rsp[:, 4:7])
            for l in range(LAYERS - 1):
                V.tensor_scalar(hb[:, l + 1:l + 2], hb[:, l + 1:l + 2], sp[0:NBLK * CH, l:l + 1], None, ALU.mult)
                V.tensor_scalar(mixw[:, l + 1, :], mixw[:, l + 1, :], rsp[0:NBLK * CH, l:l + 1], None, ALU.mult)
            for g in range(G):
                V.tensor_scalar(f1b[:, g:g + 1], f1b[:, g:g + 1], sp[:, 8 + g:9 + g], None, ALU.mult)
                V.tensor_scalar(f2w[:, g].rearrange("p a b -> p (a b)"), f2w[:, g].rearrange("p a b -> p (a b)"),
                                rsp[:, 8 + g:9 + g], None, ALU.mult)
            V.tensor_copy(half1.bitcast(F32R), raw1)
            V.drain()
            V.tensor_scalar(raw1, raw1, sg[:, 1:2], None, ALU.mult)
            V.drain()
            V.scalar_tensor_tensor(f1w[:, :], half1, sg[:, 2:3], raw1, ALU.mult, ALU.add)
            V.drain().then_inc(s_set, SETUP_V - 3)

            def normalise(t, n, i):
                V.bn_aggr(mv[:, 0:2], stats[:, :, :].rearrange("p a b -> p (a b)"))
                V.drain().then_inc(s_stin, 1)
                dve.wait_ge(s_stps, i * 4 + 2 * n + 1)
                V.tensor_copy(mv[:, 2:3], gnps[:, 0:1])
                V.drain()
                V.tensor_tensor(mv[:, 4:5], mv[:, 0:1], mv[:, 2:3], ALU.subtract)
                V.drain()
                V.tensor_tensor(mv[:, 5:6], mv[:, 4:5], mv[:, 4:5], ALU.mult)
                V.drain()
                V.tensor_tensor(mv[:, 3:4], mv[:, 5:6], mv[:, 1:2], ALU.add)
                V.drain().then_inc(s_stin, 1)
                dve.wait_ge(s_stps, i * 4 + 2 * n + 2)
                V.tensor_scalar(mv[:, 6:7], gnps[:, 1:2], EPS, None, ALU.add).then_inc(s_var, 1)
                dve.wait_ge(s_rstd, i * 2 + n + 1)
                V.tensor_scalar(zt, t, mv[:, 2:3], mv[:, 7:8], ALU.subtract, ALU.mult).then_inc(s_z, 1)

            def operand(i, c, k):
                dve.wait_ge(s_T[k], i * (NFC * 48) + c * 48 + 48)
                for half in range(2):
                    u = 2 * k + half
                    z = z3[k][:, half * 1024:half * 1024 + 1024]
                    dve.wait_ge(s_fc1, i * (24 * NFC) + c * 24 + (4 * u - 4 + HEAD))
                    V.tensor_copy(high.bitcast(F32R), z)
                    V.drain()
                    V.scalar_tensor_tensor(split[half][:, :], z, sg[:, 0:1], high, ALU.mult, ALU.subtract)
                    V.drain().then_inc(s_tm, 1)

            with dve.Fori(0, nb) as i:
                dve.wait_ge(s_x, i * 256 + 256)
                for c in range(CHUNKS):
                    V.bn_stats(stats[:, c, :], xt[:, c * 512:c * 512 + 512])
                V.drain()
                normalise(xt, 0, i)
                with dve.Fori(0, CHUNKS) as c:
                    dve.wait_ge(s_mm2, i * 8 + c + 1)
                    V.scalar_tensor_tensor(x1t[:, bass.ds(c * 512, 512)], PS[:, 2, :], c2b[:, 0:1],
                                           xt[:, bass.ds(c * 512, 512)], ALU.add, ALU.add)
                    V.drain().then_inc(s_x1, 1)
                dve.wait_ge(s_zst, i * 512 + 512)
                for c in range(CHUNKS):
                    V.bn_stats(stats[:, c, :], x1t[:, c * 512:c * 512 + 512])
                V.drain()
                normalise(x1t, 1, i)
                with dve.Fori(0, LAYERS) as l:
                    lay = i * 4 + l
                    dve.wait_ge(s_st2, lay + 1)
                    V.tensor_copy(mixl[:, :], mixw[:, bass.ds(l, 1), :].rearrange("p a b -> p (a b)"))
                    V.tensor_copy(layb[:, 0:1], hb[:, bass.ds(l + 1, 1)])
                    V.tensor_copy(layb[:, 1:2], sp[0:NBLK * CH, bass.ds(l, 1)])
                    V.tensor_scalar(fsb.rearrange("p a b -> p (a b)"), PS[:, 6, 0:480], fscale[:, bass.ds(l, 1)], None, ALU.mult)
                    V.drain()
                    dve.wait_ge(s_wsp, lay * 16 + 16)
                    for r in range(2):
                        f = fsb[:, :, 24 * r:24 * r + 24].unsqueeze(2).to_broadcast([128, WID, WID, 24])
                        V.tensor_tensor(prod.rearrange("p (i o f) -> p i o f", i=WID, o=WID),
                                        wspec[:, :].rearrange("p (i o f) -> p i o f", i=WID, o=WID), f, ALU.mult)
                        V.drain()
                        V.tensor_reduce(ot[:, 0, 0:WID, KY * r:KY * r + KY],
                                        prod.rearrange("p (i o k r) -> p o k i r", i=WID, o=WID, r=2), AXIS.XY, ALU.add)
                        V.drain()
                    V.tensor_scalar(ot[:, 1, 0:WID, 0:KY], ot[:, 0, 0:WID, KY:2 * KY], -1.0, None, ALU.mult)
                    V.tensor_copy(ot[:, 1, 0:WID, KY:2 * KY], ot[:, 0, 0:WID, 0:KY])
                    V.drain().then_inc(s_ot, 1)
                    dve.wait_ge(s_g, lay + 1)
                    for dst, src in inverse_parts(1):
                        V.tensor_copy(dst, src).then_inc(s_gD, 1)
                with dve.Fori(0, NFC) as c:
                    for k in range(NBLK):
                        operand(i, c, k)
                    dve.wait_ge(s_fc2, i * NFC + c + 1)
                    dve.wait_ge(s_xr, i * (NFC * 48) + c * 48 + 48)
                    dve.wait_ge(s_out, i * OUT_PER + c * 48)
                    V.scalar_tensor_tensor(ob, PS[0:96, 6, :], f2b[0:96, 0:1], xr, ALU.add, ALU.add).then_inc(s_fo, 1)

        @block.gpsimd
        def _(pool):
            with pool.Fori(0, nb) as i:
                for n in range(2):
                    pool.wait_ge(s_var, i * 2 + n + 1)
                    nc.gpsimd.tensor_tensor(mv[:, 7:8], mv[:, 6:7], power[:, :], ALU.pow).then_inc(s_rstd, 1)
                with pool.Fori(0, NFC) as c:
                    pool.wait_ge(s_hrow, i * 220 + 220)
                    for k in range(NBLK):
                        pool.dma_start(xr[32 * k:32 * k + 32, :],
                                       bass.AP(x1_d, c * (FCH * ROW2) + k * BSTEP * W, [[ROW2, FCH], [PIX, C], [1, ROW2]])
                                       ).then_inc(s_xr, 16)
                    pool.wait_ge(s_fo, i * NFC + c + 1)
                    nc.gpsimd.tensor_tensor(idle[:, :], power[:, :], power[:, :], ALU.add)
                    pool.drain()
                    for k in range(NBLK):
                        pool.dma_start(bass.AP(out, i * (C * PIX) + c * (FCH * ROW2) + k * BSTEP * W,
                                               [[ROW2, FCH], [PIX, C], [1, ROW2]]), ob[32 * k:32 * k + 32, :]
                                       ).then_inc(s_out, 16)
            pool.wait_ge(s_out, nb * OUT_PER)



def layouts(x, L0_conv_W1, L0_conv_b1, L0_conv_W2, L0_conv_b2, L1_conv_fc0_w, L1_conv_fc0_b, L1_conv_w_w, L1_conv_w_b,
            L1_conv_sp_w1, L1_conv_sp_w2, L1_conv_betas, L1_conv_fc1_w, L1_conv_fc1_b, L1_conv_fc2_w, L1_conv_fc2_b):
    w1, w2, b1, b2 = (np.asarray(a) for a in (L0_conv_W1, L0_conv_W2, L0_conv_b1, L0_conv_b2))
    conv1_w = np.zeros((2, 8, C, 2, HID), np.float32)
    for tap in range(9):
        if tap != 4:
            for c in range(C):
                if c * 9 + tap < 9 * C - 1:
                    for half in range(2):
                        conv1_w[half, tap - (tap > 4), c, half] = w1[c * 9 + tap]
    conv2_w = np.zeros((4, HID, 4, C), np.float32)
    for n in range(4):
        conv2_w[n, :, n] = w2
    fc0, ww = np.asarray(L1_conv_fc0_w), np.asarray(L1_conv_w_w)
    lift_w = np.zeros((28, NBLK, G, WID), np.float32)
    mix_w = np.zeros((NBLK, G, WID, LAYERS, NBLK, G, WID), np.float32)
    for k in range(NBLK):
        for g in range(G):
            for n in range(SC):
                lift_w[C * k + SC * g + n, k, g] = fc0[g, :, n]
            lift_w[C * NBLK + k, k, g] = fc0[g, :, SC]
            lift_w[C * NBLK + NBLK, k, g] = fc0[g, :, SC + 1]
            mix_w[k, g, :, :, k, g, :] = ww[:, g].transpose(2, 0, 1)
    spec = np.concatenate([np.asarray(L1_conv_sp_w1), np.asarray(L1_conv_sp_w2)], 4)
    spec_w = np.zeros((LAYERS, G, 32, WID * WID * 2 * KY), np.float32)
    spec_w[:, :, :KX] = spec.transpose(0, 1, 4, 2, 3, 5, 6).reshape(LAYERS, G, KX, -1)
    be = np.asarray(L1_conv_betas)
    betas = np.zeros((128, 12), np.float32)
    betas[:NBLK * CH, 0:4] = np.tile(np.repeat(be, WID, axis=1), (1, NBLK)).T
    betas[:, 4:8] = np.repeat(be, 32, axis=1).T
    betas[:, 8:12] = be[3][None]
    f1, f2 = np.asarray(L1_conv_fc1_w), np.asarray(L1_conv_fc2_w)
    fc1_w = np.zeros((3, G, WID, G, FF), np.float32)
    fc2_w = np.zeros((FF, G, FCH, FCH, G, SC), np.float32)
    for g in range(G):
        fc1_w[:, g, :, g, :] = f1[g].T[None]
        for n in range(FCH):
            fc2_w[:, g, n, n, g, :] = f2[g].T
    fwd_row, fwd_col, inv_row, inv_col = fourier_tables()
    return {
        "x": np.asarray(x), "conv1_w": conv1_w.reshape(128, 64), "conv1_b": np.tile(b1, 4)[:, None],
        "conv2_w": conv2_w.reshape(128, 32), "conv2_b": np.tile(b2, 16)[:, None],
        "lift_w": lift_w.reshape(28, NBLK * CH), "lift_b": np.tile(np.asarray(L1_conv_fc0_b), NBLK)[:, None],
        "mix_w": mix_w.reshape(NBLK * CH, LAYERS, NBLK * CH), "mix_b": np.tile(np.asarray(L1_conv_w_b), (1, NBLK)).T,
        "spec_w": spec_w.reshape(LAYERS, 128, -1), "betas": betas, "fc1_w": fc1_w.reshape(3 * CH, G * FF),
        "fc1_b": np.asarray(L1_conv_fc1_b).reshape(G, FF).T, "fc2_w": fc2_w.reshape(FF, G, FCH, 32),
        "fc2_b": np.tile(np.asarray(L1_conv_fc2_b), 16)[:, None], "fwd_row": fwd_row, "fwd_col": fwd_col,
        "inv_row": inv_row, "inv_col": inv_col, "grid": grid_rows(), "gmean": group_mean(), "signs": split_signs(),
    }


def kernel(**inputs):
    import concourse.bacc as bacc
    from concourse.bass_utils import run_bass_kernel_spmd

    arrays = {f"in_{k}": np.ascontiguousarray(v) for k, v in layouts(**inputs).items()}
    nc = bacc.Bacc("TRN2", target_bir_lowering=False, num_devices=1)
    args = {k[3:]: nc.dram_tensor(k, a.shape, mybir.dt.from_np(a.dtype), kind="ExternalInput")
            for k, a in arrays.items()}
    nb = arrays["in_x"].shape[0]
    out = nc.dram_tensor("out_x", arrays["in_x"].shape, F32, kind="ExternalOutput")
    ins = {k: v if k in ("x",) else v.ap() for k, v in args.items()}
    program(nc, nb, out=out, **ins)
    r = run_bass_kernel_spmd(nc, [arrays], core_ids=[0])
    return r.results[0]["out_x"]
```

```python
from contextlib import ExitStack

import numpy as np
import concourse.bass as bass
from concourse import mybir
from concourse.alu_op_type import AluOpType as ALU

F32 = mybir.dt.float32
F32R = mybir.dt.float32r
ACT = mybir.ActivationFunctionType

C, H, W = 8, 256, 256
HID = 32
G, SC, WID = 4, 2, 10
CH = G * WID
LAYERS = 4
KX, KY = 24, 12
FF = 128
PIX = H * W
ROW2 = 2 * W
PW = W + 2
PLANE = (H + 2) * PW
SPAN = 15 * PW + W
NBLK, BROWS, BSTEP = 3, 88, 84
PAIRS = BROWS // 2
BPIX = BROWS * W
CHUNKS = 8
XGRP = 4
NXG = PAIRS // XGRP
STORES = (14, 14, 12, 4)
FCH = 4
NFC = PAIRS // FCH
EPS = 1e-5
SHRINK = 1.1



def fourier_tables():
    kx = np.concatenate([np.arange(KX // 2), np.arange(-KX // 2, 0)])
    ky = np.arange(KY)
    row = 2 * np.pi / H * np.outer(np.arange(H), kx)
    col = 2 * np.pi / W * np.outer(np.arange(W), ky)
    fwd_row = np.zeros((128, 2, 64))
    fwd_row[:, :, :2 * KX] = np.concatenate([np.cos(row), -np.sin(row)], 1).reshape(2, 128, 2 * KX).transpose(1, 0, 2)
    c, s = np.cos(col), np.sin(col)
    from_re = np.concatenate([np.stack([c, s], -1).reshape(W, -1), np.stack([-s, c], -1).reshape(W, -1)], 1)
    from_im = np.concatenate([np.stack([s, -c], -1).reshape(W, -1), np.stack([c, s], -1).reshape(W, -1)], 1)
    fwd_col = np.stack([from_re, from_im], 1).reshape(2, 128, 2, 4 * KY).transpose(1, 0, 2, 3)
    inv_row = np.zeros((128, 2, H))
    for g in range(G):
        inv_row[32 * g:32 * g + KX, 0] = np.cos(row).T
        inv_row[32 * g:32 * g + KX, 1] = np.sin(row).T
    weight = np.where(ky == 0, 1.0, 2.0)[:, None] / (H * W)
    inv_col = np.zeros((128, W))
    for k in range(NBLK):
        inv_col[32 * k:32 * k + KY] = weight * c.T
        inv_col[32 * k + KY:32 * k + 2 * KY] = -weight * s.T
    f = lambda a: np.ascontiguousarray(a, np.float32)
    return f(fwd_row), f(fwd_col), f(inv_row), f(inv_col)


def grid_axes():
    return [np.linspace(0.0, 1.0, n, dtype=np.float32) for n in (H, W)]


def grid_rows():
    gx, gy = grid_axes()
    rows = [np.repeat(gx[BSTEP * k:BSTEP * k + BROWS], W) for k in range(NBLK)]
    rows += [np.tile(gy, BROWS)] + [np.zeros(BPIX)] * (32 - (C + 1) * NBLK - 1)
    return np.stack(rows).astype(np.float32)


def grid_modes():
    gx, gy = (a.astype(np.float64) for a in grid_axes())
    modes = np.zeros((G, 32, 3, 2, KY, 2))
    for n, image in enumerate((np.outer(gx, np.ones(W)), np.outer(np.ones(H), gy), np.ones((H, W)))):
        f = np.fft.rfft2(image)[:, :KY]
        f = np.concatenate([f[:KX // 2], f[-KX // 2:]])
        modes[:, :KX, n, 0] = np.stack([f.real, -f.imag], -1)
        modes[:, :KX, n, 1] = np.stack([f.imag, f.real], -1)
    return modes.reshape(128, 3, 4 * KY).astype(np.float32)


def turn_columns():
    pick = np.zeros((128, 2, 2 * KX), np.float32)
    for a in range(2):
        pick[64 * a:64 * a + 2 * KX, a] = np.eye(2 * KX)
    return pick


def group_mean():
    g = (np.arange(128) % C) // SC
    return np.where(g[:, None] == g[None], G / 128.0, 0.0).astype(np.float32)


def split_signs():
    s = np.zeros((3 * CH, 3), np.float32)
    s[CH:2 * CH, 0] = 1.0
    s[2 * CH:, 1] = -1.0
    s[:CH, 2] = -1.0
    s[CH:, 2] = 1.0
    return s


def program(nc, nb, x, conv1_w, conv1_b, conv2_w, conv2_b, lift_t, lift_b, lift_g, mix_w, mix_b, spec_w, betas,
            fc1_w, fc1_b, fc2_w, fc2_b, fwd_row, turn_id, fwd_col, inv_row, inv_col, grid, gridf, gmean, signs, out):
    with ExitStack() as ctx:
        def sb(name, shape, dt=F32):
            return ctx.enter_context(nc.sbuf_tensor(name, shape, dt))

        def sem(name):
            return ctx.enter_context(nc.semaphore(name))

        z_d = nc.dram_tensor("z_d", [C, H + 2, PW], F32, kind="Internal")
        x1_d = nc.dram_tensor("x1_d", [C, H, W], F32, kind="Internal")
        x1n_d = nc.dram_tensor("x1n_d", [C, H, W], F32, kind="Internal")
        h_d = nc.dram_tensor("h_d", [CH, H, W], F32, kind="Internal")

        hmem = sb("hmem", [128, BPIX])
        h = hmem[0:NBLK * CH, :]
        xt = hmem[:, 0:4096]
        x1t = hmem[:, 4096:8192]
        zp = hmem[:, 8192:8192 + 16 * PW]
        col = [zp, hmem[:, 8192 + 16 * PW:8192 + 32 * PW]]
        zt = hmem[:, 8192 + 32 * PW:12288 + 32 * PW]
        hid = [hmem[:, 12288 + 32 * PW + 512 * n:12800 + 32 * PW + 512 * n] for n in range(2)]
        arena = sb("arena", [128, 6144])
        himg = [arena[:, 2048 * n:2048 * n + 2048].rearrange("p (t c x) -> p t c x", t=2, c=G) for n in range(3)]
        xc = [arena[:, 2048 * n:2048 * n + 2048] for n in range(3)]
        z3 = [arena[0:3 * CH, 1024 * n:1024 * n + 1024] for n in range(3)]
        arena2 = sb("arena2", [128, 5120])
        s1 = [arena2[:, 512 * n:512 * n + 512].rearrange("p (h r m) -> p h r m", h=2, r=2) for n in range(2)]
        prod = [arena2[:, 1024 + 480 * n:1504 + 480 * n] for n in range(2)]
        acc = arena2[:, 1984:2464]
        fsb = arena2[:, 2464:2944].rearrange("p (c f) -> p c f", c=WID)
        fx = arena2[:, 2944:3040].rearrange("p (c f) -> p c f", c=SC)
        rs = [arena2[:, 3072 + 512 * n:3584 + 512 * n] for n in range(2)]
        act = [arena2[:, 1024 * n:1024 * n + 1024] for n in range(3)]
        accl = arena2[:, 4096:4576]
        wl = arena2[:, 4576:5056].rearrange("p (n f) -> p n f", n=SC)
        split = [sb(f"split{n}", [3 * CH, 1024], F32R) for n in range(2)]
        gst = sb("gst", [128, BROWS * NBLK * CH])
        gstv = gst[:, :].rearrange("p (y c) -> p y c", c=NBLK * CH)
        wspec = sb("wspec", [128, WID * WID * 2 * KY])
        xo = wspec[:, 0:NBLK * ROW2].rearrange("p (k x) -> p k x", k=NBLK)

        c1w = sb("c1w", [128, 64]); c1b = sb("c1b", [128, 1]); c2w = sb("c2w", [128, 32]); c2b = sb("c2b", [128, 1])
        compw = sb("compw", [128, NBLK * CH]); hb = sb("hb", [NBLK * CH, LAYERS])
        mixw = sb("mixw", [NBLK * CH, LAYERS - 1, NBLK * CH])
        mixl = sb("mixl", [NBLK * CH, NBLK * CH])
        layb = sb("layb", [NBLK * CH, 2])
        power = sb("power", [128, 1])
        idle = sb("idle", [128, 1])
        beta = sb("beta", [128, 12]); sp = sb("sp", [128, 12]); spt = sb("spt", [128, 12]); rsp = sb("rsp", [128, 12])
        fscale = sb("fscale", [128, LAYERS])
        f1w = sb("f1w", [3 * CH, G * FF], F32R); f1b = sb("f1b", [128, G])
        f2w = sb("f2w", [128, G, 32]); f2b = sb("f2b", [128, 1])
        fwdr = sb("fwdr", [128, 2, 64]); turn = sb("turn", [128, 2, 2 * KX]); fwdc = sb("fwdc", [128, 2, 2, 4 * KY])
        invr = sb("invr", [128, 2, H]); invc = sb("invc", [128, W])
        gm = sb("gm", [128, 128]); sg = sb("sg", [3 * CH, 3])
        stats = sb("stats", [128, CHUNKS, 6]); mv = sb("mv", [128, 8])
        ot = sb("ot", [128, 2, 12, 32])

        PS = ctx.enter_context(nc.psum_tensor("PS", [128, 8, 512], F32))
        gnps = PS[:, 7, :]

        s_w = sem("weights_loaded"); s_set = sem("setup_vector"); s_sact = sem("setup_scalar")
        s_zero = sem("border_zeroed")
        s_x = sem("x_loaded"); s_stin = sem("stats_in"); s_stps = sem("stats_summed"); s_var = sem("variance")
        s_rstd = sem("rstd"); s_z = sem("z_ready"); s_zst = sem("z_stored")
        s_set0 = sem("setup_products"); s_fev = sem("modes_taken")
        s_col = [sem("col0_loaded"), sem("col1_loaded")]
        s_mm1 = sem("conv1_done"); s_relu = sem("relu_done"); s_mm2 = sem("conv2_done"); s_x1 = sem("x1_chunk")
        s_x1st = sem("x1_stored"); s_x1nst = sem("x1_normalised_stored")
        s_xc = [sem(f"lift{n}_loaded") for n in range(3)]
        s_row = sem("rows_summed"); s_hrow = sem("rows_ready"); s_hst = sem("h_stored")
        s_himg = [sem(f"image{n}_loaded") for n in range(3)]
        s_wsp = sem("spectral_weights"); s_pad = sem("lift_padded")
        s_st1 = sem("row_transform"); s_rs = sem("row_transform_copied"); s_turn = sem("row_transform_turned")
        s_s1ev = sem("row_transform_kept"); s_st2 = sem("column_transform")
        s_ot = sem("modes_mixed"); s_g = sem("inverse_rows"); s_gA = sem("inverse_rows_kept_scalar")
        s_gD = sem("inverse_rows_kept_vector")
        s_T = [sem(f"z3_{k}_loaded") for k in range(3)]
        s_tm = sem("operand_split"); s_fc1 = sem("fc1_done"); s_silu = sem("silu_done"); s_fc2 = sem("fc2_done")
        s_xr = sem("residual_loaded"); s_fo = sem("result_ready"); s_out = sem("result_stored")

        HEAD, HEAD_MM1, HEAD_X1, HEAD_TM, HEAD_FO, HEAD_OUT = 8, 8, 1, 3, 3, 1
        ROWS = LAYERS * PAIRS
        ST = SC + (LAYERS - 1) * WID
        UNITS = NFC * NBLK
        raw1 = arena[0:3 * CH, 0:G * FF]
        half1 = arena[0:3 * CH, G * FF:2 * G * FF]
        liftt = arena[0:NBLK * CH, 1024:1152]
        liftb = arena[0:NBLK * CH, 1152:1153]
        mixw0 = arena[0:NBLK * CH, 1160:1160 + NBLK * CH]
        gridm = arena[:, 1280:1424].rearrange("p (n f) -> p n f", n=3)
        term = arena[:, 1424:1904].rearrange("p (c f) -> p c f", c=WID)
        lg = arena[:, 1904:1904 + (SC + 3) * WID].rearrange("p (n c) -> p n c", n=SC + 3)
        consts = [(c1w[:, :], conv1_w), (c1b[:, :], conv1_b), (c2w[:, :], conv2_w), (c2b[:, :], conv2_b),
                  (liftt, lift_t), (liftb, lift_b), (lg, lift_g), (gridm, gridf), (hb[:, :], mix_b),
                  (mixw0, mix_w[:, 0, :]), (mixw[:, :, :], mix_w[:, 1:, :]),
                  (beta[:, :], betas), (arena[0:3 * CH, 0:G * FF], fc1_w), (f1b[:, :], fc1_b), (f2w[:, :, :], fc2_w),
                  (f2b[:, :], fc2_b), (fwdr[:, :, :], fwd_row), (turn[:, :, :], turn_id),
                  (fwdc[:, :, :, :], fwd_col), (invr[:, :, :], inv_row), (invc[:, :], inv_col), (gm[:, :], gmean), (sg[:, :], signs)]
        SETUP_V = 5
        HST = 16 * sum(1 for q, n in enumerate(STORES) for k in range(NBLK)
                       if min(2 * n, (BSTEP if k < NBLK - 1 else BROWS) - 2 * sum(STORES[:q])) > 0)

        def inverse_parts(n, gh):
            gs = slice(2 * gh, 2 * gh + 2)
            parts = []
            for slot in (n, n + 2):
                for k in range(NBLK):
                    y = BSTEP * k
                    src = PS[32 * slot:32 * slot + 2 * KY, gs, :].rearrange("p g (s y) -> p g s y", s=2)
                    dst = gstv[32 * k:32 * k + 2 * KY, :, CH * k:CH * k + CH].rearrange("p y (g o) -> p g o y", g=G)
                    parts.append((dst[:, gs, slot:slot + 5:4, :], src[:, :, :, y:y + BROWS]))
                    if slot < 2:
                        parts.append((dst[:, gs, 8 + slot, :],
                                      PS[32 * slot:32 * slot + 2 * KY, 4 + 2 * gh:6 + 2 * gh, y:y + BROWS]))
            return parts

        GP = [2 * len(inverse_parts(n, 0)) for n in range(2)]

        def himg_uses(b, i, l, n):
            per = (WID + 2 - b) // 3
            first = 1 if b < SC else 0
            if l is None:
                return i * (first + (LAYERS - 1) * per) + 1
            return i * (first + (LAYERS - 1) * per) + (l - 1) * per + (first + n + 1)

        block = ctx.enter_context(nc.Block())

        def pieces(dram, img, m):
            return [bass.AP(dram, img + half * 128 * W + m * ROW2, [[PIX, C], [16 * W, CHUNKS], [1, ROW2]])
                    for half in range(2)]

        @block.sync
        def _(sp_):
            for dst, src in consts:
                sp_.dma_start(dst, src).then_inc(s_w, 16)
            sp_.dma_start(wspec[:, :], spec_w[0, :, :]).then_inc(s_wsp, 16)
            sp_.wait_ge(s_set, 1)
            sp_.dma_start(bass.AP(z_d, 0, [[PLANE, C], [(H + 1) * PW, 2], [1, PW]]),
                          gst[0:C, 0:2 * PW].rearrange("p (a b) -> p a b", a=2)).then_inc(s_zero, 16)
            sp_.wait_ge(s_zero, 16)
            with sp_.Fori(0, nb) as i:
                sp_.wait_ge(s_tm, i * 66 + HEAD_TM)
                for m in range(8):
                    for half, src in enumerate(pieces(x, i * (C * PIX), m)):
                        p = 16 * m + 8 * half
                        sp_.dma_start(xt[p:p + 8, :].rearrange("p (a b) -> p a b", a=CHUNKS), src).then_inc(s_x, 16)
                sp_.wait_ge(s_z, i * 2 + 1)
                for m in range(8):
                    for half in range(2):
                        p = 16 * m + 8 * half
                        dst = bass.AP(z_d, (128 * half + 2 * m + 1) * PW, [[PLANE, C], [16 * PW, CHUNKS], [1, 2 * PW]])
                        sp_.dma_start(dst, zp[p:p + 8, :].rearrange("p (a b) -> p a b", a=CHUNKS)).then_inc(s_zst, 16)
                with sp_.Fori(0, CHUNKS // 2) as j:
                    for par in range(2):
                        if par == 0:
                            sp_.wait_ge(s_zst, i * 256 + 256)
                        sp_.wait_ge(s_mm1, i * 32 + (j * 2 + par) * 4 + (HEAD_MM1 - 4))
                        for half in range(2):
                            for dy, first, shifts, step in ((0, 0, 3, 1), (1, 24, 2, 2), (2, 40, 3, 1)):
                                p = 64 * half + first
                                at = (j * 2 + par) * (16 * PW) + (128 * half + dy) * PW
                                sp_.dma_start(col[par][p:p + 8 * shifts, 0:SPAN],
                                              bass.AP(z_d, at, [[step, shifts], [PLANE, C], [1, SPAN]])
                                              ).then_inc(s_col[par], 16)
                sp_.wait_ge(s_z, i * 2 + 2)
                for m in range(8):
                    for half, dst in enumerate(pieces(x1n_d, 0, m)):
                        p = 16 * m + 8 * half
                        sp_.dma_start(dst, zt[p:p + 8, :].rearrange("p (a b) -> p a b", a=CHUNKS)).then_inc(s_x1nst, 16)
                sp_.wait_ge(s_x1nst, i * 256 + 256)
                for n in range(SC):
                    for t in range(2):
                        sp_.dma_start(himg[n][:, t], bass.AP(x1n_d, n * PIX + t * 128 * W, [[W, 128], [SC * PIX, G], [1, W]])
                                      ).then_inc(s_himg[n], 16)
                sp_.wait_ge(s_out, i * (NFC * 64) + HEAD_OUT)
                for m in range(8):
                    for half, dst in enumerate(pieces(x1_d, 0, m)):
                        p = 16 * m + 8 * half
                        sp_.dma_start(dst, x1t[p:p + 8, :].rearrange("p (a b) -> p a b", a=CHUNKS)).then_inc(s_x1st, 16)
                with sp_.Fori(1, LAYERS) as l:
                    sp_.wait_ge(s_ot, i * 4 + l)
                    sp_.dma_start(wspec[:, :], spec_w[bass.ds(l, 1), :, :].rearrange("a p n -> (a p) n")).then_inc(s_wsp, 16)
                    for q, n in enumerate(STORES):
                        y0 = 2 * sum(STORES[:q])
                        sp_.wait_ge(s_hrow, i * ROWS + l * PAIRS + (sum(STORES[:q + 1]) - PAIRS))
                        for k in range(NBLK):
                            rows = min(2 * n, (BSTEP if k < NBLK - 1 else BROWS) - y0)
                            if rows > 0:
                                sp_.dma_start(bass.AP(h_d, (BSTEP * k + y0) * W, [[PIX, CH], [1, rows * W]]),
                                              hmem[CH * k:CH * k + CH, y0 * W:(y0 + rows) * W]).then_inc(s_hst, 16)
                    sp_.wait_ge(s_hst, (i * 3 + l - 1) * HST + HST)
                    for c in range(WID):
                        if c >= 3:
                            sp_.wait_ge(s_st1, i * ST + (l - 1) * WID + (SC + c - 2))
                        for t in range(2):
                            sp_.dma_start(himg[c % 3][:, t],
                                          bass.AP(h_d, c * PIX + t * 128 * W, [[W, 128], [WID * PIX, G], [1, W]])
                                          ).then_inc(s_himg[c % 3], 16)
                first_chunk = 0

                def operands(c):
                    for u in range(2 * NBLK):
                        k, half = divmod(u, 2)
                        if c is not first_chunk or u >= 3:
                            sp_.wait_ge(s_tm, i * 66 + c * 6 + (u - 2 + HEAD_TM))
                        elif u == 0:
                            sp_.wait_ge(s_hrow, i * ROWS + ROWS)
                        for r in range(3):
                            sp_.dma_start(z3[u % 3][CH * r:CH * r + CH, :],
                                          hmem[CH * k:CH * k + CH, bass.ds(c * (FCH * ROW2), FCH * ROW2)].rearrange(
                                              "p (n h x) -> p h n x", n=FCH, h=2)[:, half]).then_inc(s_T[u % 3], 16)

                def rows_of(dram, start, c, n):
                    return bass.AP(dram, start + c * (FCH * ROW2) + n * ROW2, [[PIX, C], [BSTEP * W, NBLK], [1, ROW2]])

                def residual(c):
                    for n in range(FCH):
                        sp_.dma_start(xo[32 * n:32 * n + C], rows_of(x1_d, 0, c, n)).then_inc(s_xr, 16)

                def store(c):
                    sp_.wait_ge(s_fo, i * UNITS + c * 3 + (NBLK + HEAD_FO))
                    for n in range(FCH):
                        sp_.dma_start(rows_of(out, i * (C * PIX), c, n), xo[32 * n:32 * n + C]).then_inc(s_out, 16)

                operands(first_chunk)
                residual(first_chunk)
                with sp_.Fori(1, NFC) as c:
                    operands(c)
                    store(c - 1)
                    sp_.wait_ge(s_out, i * (NFC * 64) + c * 64 + HEAD_OUT)
                    residual(c)
                store(NFC - 1)
            sp_.wait_ge(s_out, nb * (NFC * 64) + HEAD_OUT)

        @block.tensor
        def _(pe):
            pe.wait_ge(s_w, 16 * len(consts))
            pe.wait_ge(s_set, 1)
            nc.tensor.matmul(PS[:, 0, 0:NBLK * CH], liftt, mixw0, start=True, stop=True)
            nc.tensor.matmul(PS[0:NBLK * CH, 1, 0:1], mixw0, liftb, start=True, stop=True).then_inc(s_set0, 1)
            pe.wait_ge(s_set, SETUP_V)
            pe.sem_inc(s_fc1, HEAD)
            pe.sem_inc(s_mm1, HEAD_MM1)
            with pe.Fori(0, nb) as i:
                def group_sums(n):
                    for r in range(2):
                        pe.wait_ge(s_stin, i * 4 + 2 * n + r + 1)
                        nc.tensor.matmul(gnps[:, r:r + 1], gm[:, :], mv[:, 3 * r:3 * r + 1],
                                         start=True, stop=True).then_inc(s_stps, 1)

                group_sums(0)
                with pe.Fori(0, CHUNKS // 2) as j:
                    for par in range(2):
                        chunk = i * 8 + j * 2 + par
                        pe.wait_ge(s_col[par], (i * 4 + j + 1) * 96)

                        def second(q):
                            pe.wait_ge(s_relu, chunk * 4 + q + 1)
                            if q == 0:
                                pe.wait_ge(s_x1, chunk + HEAD_X1)
                            mm = nc.tensor.matmul(PS[32 * q:32 * q + 32, 2, :], c2w[:, :], hid[q % 2],
                                                  start=True, stop=True, tile_position=(0, 32 * q))
                            if q == 3:
                                mm.then_inc(s_mm2, 1)

                        for q in range(4):
                            for u in range(2):
                                y = 2 * (2 * q + u)
                                mm = nc.tensor.matmul(PS[64 * u:64 * u + 64, q % 2, :], c1w[:, :],
                                                      col[par].rearrange("p (y x) -> p y x", x=PW)[:, y:y + 2, 0:W],
                                                      start=True, stop=True, tile_position=(0, 64 * u))
                            mm.then_inc(s_mm1, 1)
                            if q:
                                second(q - 1)
                        second(3)
                group_sums(1)

                def row_transform(c, uses, done):
                    pe.wait_ge(s_himg[c % 3], uses * 32)
                    if c >= 2:
                        pe.wait_ge(s_rs, done + (c - 1))
                    for t in range(2):
                        for a in range(2):
                            mm = nc.tensor.matmul(PS[64 * a:64 * a + 64, 6 + c % 2, :], fwdr[:, t, :],
                                                  himg[c % 3][:, t, 2 * a:2 * a + 2, :].rearrange("p g x -> p (g x)"),
                                                  start=t == 0, stop=t == 1, tile_position=(0, 64 * a))
                    mm.then_inc(s_st1, 1)

                def turned(c, done):
                    pe.wait_ge(s_rs, done + (c + 1))
                    if c >= 2:
                        pe.wait_ge(s_s1ev, (done + (c - 1)) * 2)
                    for xh in range(2):
                        to = PS[:, 4 + c % 2, xh * 192:xh * 192 + 192].rearrange("p (a b m) -> p b a m", a=2, b=2)
                        for b in range(2):
                            mm = nc.tensor.matmul(to[:, b], rs[c % 2][:, 256 * b + 128 * xh:256 * b + 128 * xh + 128],
                                                  turn[:, :, :], start=True, stop=True)
                    mm.then_inc(s_turn, 1)

                def column_transform(c, done):
                    pe.wait_ge(s_s1ev, (done + (c + 1)) * 2)
                    if c >= 4:
                        pe.wait_ge(s_fev, done + (c - 3))
                    for n in range(4):
                        xh, r = divmod(n, 2)
                        mm = nc.tensor.matmul(PS[:, c % 4, 0:48], s1[c % 2][:, xh, r, :], fwdc[:, xh, r, :],
                                              start=n == 0, stop=n == 3)
                    mm.then_inc(s_st2, 1)

                def inverse_rows(lay):
                    pe.wait_ge(s_ot, lay + 1)
                    for g in range(G):
                        for s in (2, 0, 1):
                            bank, at = (4 + g, 0) if s == 2 else (g, 256 * s)
                            for cs in range(2):
                                mm = nc.tensor.matmul(PS[:, bank, at:at + 256],
                                                      ot[32 * g:32 * g + 32, cs, 4 * s:4 * s + 4, :].rearrange("p a b -> p (a b)"),
                                                      invr[32 * g:32 * g + 32, cs, :], start=cs == 0, stop=cs == 1,
                                                      tile_position=(32 * g, 0))
                        if g % 2:
                            mm.then_inc(s_g, 1)
                    pe.wait_ge(s_gA, lay * GP[0] + GP[0])
                    pe.wait_ge(s_gD, lay * GP[1] + GP[1])

                def back_to_pixels(p):
                    for r in range(2):
                        mm = nc.tensor.matmul(PS[0:NBLK * CH, p % 4, r * W:r * W + W], gstv[:, 2 * p + r, :], invc[:, :],
                                              start=False, stop=True, skip_group_check=True)
                    mm.then_inc(s_row, 1)

                for c in range(SC + 2):
                    if c < SC:
                        row_transform(c, himg_uses(c, i, None, 0), i * ST)
                    if 1 <= c <= SC:
                        turned(c - 1, i * ST)
                    if c >= 2:
                        column_transform(c - 2, i * ST)
                inverse_rows(i * 4)
                pe.wait_ge(s_pad, i + 1)
                for p in range(PAIRS):
                    q = p // XGRP
                    if p % XGRP == 0:
                        pe.wait_ge(s_xc[q % 3], (i * len(range(q % 3, NXG, 3)) + (q // 3 + 1)) * 64)
                    if p >= 4:
                        pe.wait_ge(s_hrow, i * ROWS + (p - 3))
                    nc.tensor.matmul(PS[0:NBLK * CH, p % 4, :], compw[:, :],
                                     xc[q % 3][:, (p % XGRP) * ROW2:(p % XGRP + 1) * ROW2], start=True, stop=True)
                    back_to_pixels(p)

                with pe.Fori(1, LAYERS) as l:
                    done = i * ST + (l - 1) * WID + SC
                    for c in range(WID + 2):
                        if c < WID:
                            row_transform(c, himg_uses(c % 3, i, l, c // 3), done)
                        if 1 <= c <= WID:
                            turned(c - 1, done)
                        if c >= 2:
                            column_transform(c - 2, done)
                    inverse_rows(i * 4 + l)
                    for p in range(PAIRS):
                        if p >= 4:
                            pe.wait_ge(s_hrow, i * ROWS + l * PAIRS + (p - 3))
                        nc.tensor.matmul(PS[0:NBLK * CH, p % 4, :], mixl[:, :], h[:, p * ROW2:(p + 1) * ROW2],
                                         start=True, stop=True)
                        back_to_pixels(p)

                def fc1(c, s):
                    u, g = divmod(s, G)
                    if g == 0:
                        pe.wait_ge(s_tm, i * 66 + c * 6 + (u + 1 + HEAD_TM))
                    for p in range(2):
                        mm = nc.tensor.matmul(PS[:, 2 * (s % 3) + p, :], f1w[:, g * FF:g * FF + FF],
                                              split[u % 2][:, p * 512:p * 512 + 512], start=True, stop=True)
                    mm.then_inc(s_fc1, 1)

                def fc2(c, s):
                    u, g = divmod(s, G)
                    k, half = divmod(u, 2)
                    pe.wait_ge(s_silu, i * (24 * NFC) + c * 24 + (s + 1))
                    if s % 8 == 0:
                        pe.wait_ge(s_fo, i * UNITS + c * 3 + ((0, -1, 1)[k] + HEAD_FO))
                    for n in range(FCH):
                        mm = nc.tensor.matmul(PS[32 * n:32 * n + 32, 6 + k % 2, half * W:half * W + W], f2w[:, g, :],
                                              act[s % 3][:, n * W:n * W + W],
                                              start=g == 0, stop=g == G - 1, tile_position=(0, 32 * n))
                    if s % 8 == 7:
                        mm.then_inc(s_fc2, 1)

                for s in range(3):
                    fc1(0, s)
                with pe.Fori(0, NFC - 1) as c:
                    for s in range(24):
                        fc2(c, s)
                        fc1(c, s + 3) if s < 21 else fc1(c + 1, s - 21)
                for s in range(24):
                    fc2(NFC - 1, s)
                    if s < 21:
                        fc1(NFC - 1, s + 3)

        @block.scalar
        def _(act_):
            act_.wait_ge(s_w, 16 * len(consts))
            act_.wait_ge(s_set, 2)
            nc.scalar.activation(rsp[:, :], spt[:, :], ACT.Exp).then_inc(s_sact, 1)
            act_.wait_ge(s_set, 3)
            nc.scalar.activation(spt[:, :], sp[:, :], ACT.Ln).then_inc(s_sact, 1)
            act_.wait_ge(s_set, SETUP_V)

            def rows(lead, bias, scale, func):
                for p in range(PAIRS):
                    act_.wait_ge(s_row, lead + (p + 1))
                    nc.scalar.activation(h[:, p * ROW2:(p + 1) * ROW2], PS[0:NBLK * CH, p % 4, :], func,
                                         bias=bias, scale=scale).then_inc(s_hrow, 1)

            def transforms(count, done, lay):
                for c in range(count + 1):
                    if c < count:
                        act_.wait_ge(s_st1, done + (c + 1))
                        nc.scalar.activation(rs[c % 2], PS[:, 6 + c % 2, :], ACT.Identity).then_inc(s_rs, 1)
                    if c == 0:
                        continue
                    act_.wait_ge(s_turn, done + c)
                    for xh in range(2):
                        src = PS[:, 4 + (c - 1) % 2, xh * 192:xh * 192 + 192].rearrange("p (g r k) -> p r g k", g=G, r=2)
                        dst = s1[(c - 1) % 2][:, xh].rearrange("p r (g m) -> p r g m", g=G)[:, :, :, 0:KX]
                        nc.scalar.activation(dst, src, ACT.Identity).then_inc(s_s1ev, 1)
                for gh in range(2):
                    act_.wait_ge(s_g, lay * 2 + (gh + 1))
                    for e in inverse_parts(0, gh):
                        nc.scalar.activation(*e, ACT.Identity).then_inc(s_gA, 1)

            with act_.Fori(0, nb) as i:
                with act_.Fori(0, CHUNKS // 2) as j:
                    for n in range(8):
                        act_.wait_ge(s_mm1, i * 32 + j * 8 + (n + 1 + HEAD_MM1))
                        nc.scalar.activation(hid[n % 2], PS[:, n % 2, :], ACT.Relu, bias=c1b[:, 0:1]).then_inc(s_relu, 1)
                transforms(SC, i * ST, i * 4)
                act_.wait_ge(s_x1st, i * 256 + 256)
                rows(i * ROWS, layb[:, 0:1], layb[:, 1:2], ACT.Silu)
                with act_.Fori(1, LAYERS - 1) as l:
                    transforms(WID, i * ST + (l - 1) * WID + SC, i * 4 + l)
                    rows(i * ROWS + l * PAIRS, layb[:, 0:1], layb[:, 1:2], ACT.Silu)
                transforms(WID, i * ST + (LAYERS - 2) * WID + SC, i * 4 + (LAYERS - 1))
                rows(i * ROWS + (LAYERS - 1) * PAIRS, hb[:, LAYERS - 1:LAYERS], 1.0, ACT.Identity)
                with act_.Fori(0, NFC) as c:
                    for s in range(24):
                        g = s % G
                        act_.wait_ge(s_fc1, i * (24 * NFC) + c * 24 + (s + 1 + HEAD))
                        pair = 2 * (s % 3)
                        nc.scalar.activation(act[s % 3], PS[:, pair:pair + 2, :].rearrange("p a b -> p (a b)"), ACT.Silu,
                                             bias=f1b[:, g:g + 1], scale=sp[:, 8 + g:9 + g]).then_inc(s_silu, 1)

        @block.vector
        def _(dve):
            V = nc.vector

            def products(dst, w, f):
                V.tensor_tensor(dst.rearrange("p (r o f) -> p r o f", r=2, o=WID),
                                w.rearrange("p (o f) -> p o f", o=WID).unsqueeze(1).to_broadcast([128, 2, WID, 2 * KY]),
                                f.rearrange("p (r f) -> p r f", r=2).unsqueeze(2).to_broadcast([128, 2, WID, 2 * KY]),
                                ALU.mult)

            def mix(c, first):
                products(acc if first else prod[c % 2], wspec[:, c * 240:c * 240 + 240], fsb[:, c, :])
                V.drain()
                if not first:
                    V.tensor_tensor(acc, acc, prod[c % 2], ALU.add)
                    V.drain()

            dve.sem_inc(s_tm, HEAD_TM)
            dve.sem_inc(s_x1, HEAD_X1)
            dve.sem_inc(s_out, HEAD_OUT)
            dve.sem_inc(s_fo, HEAD_FO)
            V.memset(gst[:, :], 0.0)
            V.memset(arena2[:, :], 0.0)
            V.memset(ot[:, :, :, :], 0.0)
            V.memset(power[:, :], -0.5)
            V.drain().then_inc(s_set, 1)
            dve.wait_ge(s_w, 16 * len(consts))
            V.tensor_scalar(sp[:, :], beta[:, :], -1.0, None, ALU.mult)
            V.drain()
            V.tensor_tensor(spt[:, :], beta[:, :], sp[:, :], ALU.min)
            V.drain().then_inc(s_set, 1)
            dve.wait_ge(s_sact, 1)
            V.tensor_scalar(sp[:, :], rsp[:, :], 1.0, None, ALU.add)
            V.drain().then_inc(s_set, 1)
            dve.wait_ge(s_sact, 2)
            V.tensor_scalar(sp[:, :], beta[:, :], 0.0, None, ALU.max)
            V.drain()
            V.tensor_tensor(sp[:, :], sp[:, :], spt[:, :], ALU.add)
            V.drain()
            V.tensor_scalar(sp[:, :], sp[:, :], 1e-20, SHRINK, ALU.max, ALU.mult)
            V.drain()
            V.reciprocal(rsp[:, :], sp[:, :])
            V.tensor_scalar(sp[:, :], sp[:, :], 1.0 / SHRINK, None, ALU.mult)
            V.drain()
            V.memset(fscale[:, 0:1], 1.0)
            dve.wait_ge(s_set0, 1)
            V.tensor_copy(compw[:, :], PS[:, 0, 0:NBLK * CH])
            V.tensor_tensor(hb[:, 0:1], PS[0:NBLK * CH, 1, 0:1], hb[:, 0:1], ALU.add)
            for n in range(3):
                dst = term if n else fsb
                V.tensor_tensor(dst, lg[:, SC + n, :].unsqueeze(2).to_broadcast([128, WID, 4 * KY]),
                                gridm[:, n, :].unsqueeze(1).to_broadcast([128, WID, 4 * KY]), ALU.mult)
                V.drain()
                if n:
                    V.tensor_tensor(fsb, fsb, term, ALU.add)
                    V.drain()
            dve.wait_ge(s_wsp, 16)
            for c in range(WID):
                mix(c, c == 0)
                for n in range(SC):
                    w = wspec[:, c * 240:c * 240 + 240]
                    if c:
                        V.scalar_tensor_tensor(wl[:, n], w, lg[:, n, c:c + 1], wl[:, n], ALU.mult, ALU.add)
                    else:
                        V.tensor_scalar(wl[:, n], w, lg[:, n, c:c + 1], None, ALU.mult)
                V.drain()
            V.tensor_copy(accl, acc)
            V.tensor_copy(fscale[:, 1:LAYERS], rsp[:, 4:7])
            for l in range(LAYERS - 1):
                V.tensor_scalar(hb[:, l:l + 1], hb[:, l:l + 1], sp[0:NBLK * CH, l:l + 1], None, ALU.mult)
                V.tensor_scalar(mixw[:, l, :], mixw[:, l, :], rsp[0:NBLK * CH, l:l + 1], None, ALU.mult)
            for g in range(G):
                V.tensor_scalar(f1b[:, g:g + 1], f1b[:, g:g + 1], sp[:, 8 + g:9 + g], None, ALU.mult)
                V.tensor_scalar(f2w[:, g], f2w[:, g],
                                rsp[:, 8 + g:9 + g], None, ALU.mult)
            V.tensor_copy(half1.bitcast(F32R), raw1)
            V.drain()
            V.tensor_scalar(raw1, raw1, sg[:, 1:2], None, ALU.mult)
            V.drain()
            V.scalar_tensor_tensor(f1w[:, :], half1, sg[:, 2:3], raw1, ALU.mult, ALU.add)
            V.drain().then_inc(s_set, SETUP_V - 3)

            def normalise(t, n, i):
                V.bn_aggr(mv[:, 0:2], stats[:, :, :].rearrange("p a b -> p (a b)"))
                V.drain().then_inc(s_stin, 1)
                dve.wait_ge(s_stps, i * 4 + 2 * n + 1)
                V.tensor_copy(mv[:, 2:3], gnps[:, 0:1])
                V.drain()
                V.tensor_tensor(mv[:, 4:5], mv[:, 0:1], mv[:, 2:3], ALU.subtract)
                V.drain()
                V.tensor_tensor(mv[:, 5:6], mv[:, 4:5], mv[:, 4:5], ALU.mult)
                V.drain()
                V.tensor_tensor(mv[:, 3:4], mv[:, 5:6], mv[:, 1:2], ALU.add)
                V.drain().then_inc(s_stin, 1)
                dve.wait_ge(s_stps, i * 4 + 2 * n + 2)
                V.tensor_scalar(mv[:, 6:7], gnps[:, 1:2], EPS, None, ALU.add).then_inc(s_var, 1)
                dve.wait_ge(s_rstd, i * 2 + n + 1)
                norm = (mv[:, 2:3], mv[:, 7:8], ALU.subtract, ALU.mult)
                if n:
                    V.tensor_scalar(zt, t, *norm).then_inc(s_z, 1)
                    return
                padded = zp.rearrange("p (y x) -> p y x", x=PW)
                V.memset(padded[:, :, 0:1], 0.0)
                V.memset(padded[:, :, PW - 1:PW], 0.0)
                V.tensor_scalar(padded[:, :, 1:W + 1], t.rearrange("p (y x) -> p y x", x=W), *norm)
                V.drain().then_inc(s_z, 1)

            def operand(i, c, k):
                for u in (2 * k, 2 * k + 1):
                    dve.wait_ge(s_T[u % 3], i * (NFC * 96) + c * 96 + (48 + u // 3 * 48))
                    dve.wait_ge(s_fc1, i * (24 * NFC) + c * 24 + (4 * u - 4 + HEAD))
                    V.tensor_copy(split[u % 2][:, :], z3[u % 3])
                    V.drain()
                    V.scalar_tensor_tensor(split[u % 2][:, :], z3[u % 3], sg[:, 0:1], split[u % 2][:, :].bitcast(F32),
                                           ALU.mult, ALU.subtract)
                    V.drain().then_inc(s_tm, 1)

            def result(i, c, k):
                dve.wait_ge(s_fc2, i * UNITS + c * 3 + (k + 1))
                if k == 0:
                    dve.wait_ge(s_xr, i * (NFC * 64) + c * 64 + 64)
                V.scalar_tensor_tensor(xo[:, k], PS[:, 6 + k % 2, :], f2b[:, 0:1], xo[:, k], ALU.add, ALU.add
                                       ).then_inc(s_fo, 1)

            def layer_constants(l):
                V.tensor_copy(layb[:, 0:1], hb[:, bass.ds(l, 1)])
                V.tensor_copy(layb[:, 1:2], sp[0:NBLK * CH, bass.ds(l, 1)])

            def mixed():
                pairs = acc.rearrange("p (r o k s) -> p r o k s", r=2, o=WID, s=2)
                for r in range(2):
                    V.tensor_tensor(ot[:, 0, 0:WID, KY * r:KY * r + KY], pairs[:, r, :, :, 0], pairs[:, r, :, :, 1], ALU.add)
                V.drain()
                V.tensor_scalar(ot[:, 1, 0:WID, 0:KY], ot[:, 0, 0:WID, KY:2 * KY], -1.0, None, ALU.mult)
                V.tensor_copy(ot[:, 1, 0:WID, KY:2 * KY], ot[:, 0, 0:WID, 0:KY])
                V.drain().then_inc(s_ot, 1)

            def inverse_kept(lay):
                for gh in range(2):
                    dve.wait_ge(s_g, lay * 2 + (gh + 1))
                    for dst, src in inverse_parts(1, gh):
                        V.tensor_copy(dst, src).then_inc(s_gD, 1)

            with dve.Fori(0, nb) as i:
                dve.wait_ge(s_x, i * 256 + 256)
                for c in range(CHUNKS):
                    V.bn_stats(stats[:, c, :], xt[:, c * 512:c * 512 + 512])
                V.drain()
                normalise(xt, 0, i)
                with dve.Fori(0, CHUNKS) as c:
                    dve.wait_ge(s_mm2, i * 8 + c + 1)
                    V.scalar_tensor_tensor(x1t[:, bass.ds(c * 512, 512)], PS[:, 2, :], c2b[:, 0:1],
                                           xt[:, bass.ds(c * 512, 512)], ALU.add, ALU.add)
                    V.drain().then_inc(s_x1, 1)
                    V.bn_stats(stats[:, bass.ds(c, 1), :].rearrange("p a b -> p (a b)"), x1t[:, bass.ds(c * 512, 512)])
                V.drain()
                normalise(x1t, 1, i)
                layer_constants(0)
                for c in range(SC):
                    dve.wait_ge(s_st2, i * ST + c + 1)
                    V.tensor_copy(fx[:, c, :], PS[:, c, 0:48]).then_inc(s_fev, 1)
                V.drain()
                for n in range(SC):
                    products(prod[n], wl[:, n], fx[:, n, :])
                V.drain()
                V.tensor_tensor(acc, accl, prod[0], ALU.add)
                V.drain()
                V.tensor_tensor(acc, acc, prod[1], ALU.add)
                V.drain()
                mixed()
                inverse_kept(i * 4)
                with dve.Fori(1, LAYERS) as l:
                    dve.wait_ge(s_hrow, i * ROWS + l * PAIRS)
                    V.tensor_copy(mixl[:, :], mixw[:, bass.ds(l - 1, 1), :].rearrange("p a b -> p (a b)"))
                    layer_constants(l)
                    dve.wait_ge(s_wsp, i * 48 + l * 16 + 16)
                    for c in range(WID):
                        dve.wait_ge(s_st2, i * ST + (l - 1) * WID + (SC + c + 1))
                        V.tensor_scalar(fsb[:, c, :], PS[:, c % 4, 0:48], fscale[:, bass.ds(l, 1)], None,
                                        ALU.mult).then_inc(s_fev, 1)
                        V.drain()
                        mix(c, c == 0)
                    mixed()
                    inverse_kept(i * 4 + l)
                operand(i, 0, 0)
                with dve.Fori(0, NFC - 1) as c:
                    operand(i, c, 1)
                    result(i, c, 0)
                    operand(i, c, 2)
                    result(i, c, 1)
                    operand(i, c + 1, 0)
                    result(i, c, 2)
                operand(i, NFC - 1, 1)
                result(i, NFC - 1, 0)
                operand(i, NFC - 1, 2)
                result(i, NFC - 1, 1)
                result(i, NFC - 1, 2)

        @block.gpsimd
        def _(pool):
            with pool.Fori(0, nb) as i:
                for n in range(2):
                    pool.wait_ge(s_var, i * 2 + n + 1)
                    nc.gpsimd.tensor_tensor(mv[:, 7:8], mv[:, 6:7], power[:, :], ALU.pow).then_inc(s_rstd, 1)


                def carry_wait():
                    nc.gpsimd.tensor_tensor(idle[:, :], power[:, :], power[:, :], ALU.add)
                    pool.drain()

                pool.wait_ge(s_st1, i * ST + SC)
                carry_wait()
                nc.gpsimd.memset(arena[32:64, :], 0.0)
                nc.gpsimd.memset(arena[64:128, :], 0.0)
                pool.drain().then_inc(s_pad, 1)
                for q in range(NXG):
                    if q > 2:
                        pool.wait_ge(s_row, i * ROWS + XGRP * (q - 2))
                        carry_wait()
                    for k in range(NBLK):
                        pool.dma_start(xc[q % 3][8 * k:8 * k + 8, :],
                                       bass.AP(x1n_d, q * (XGRP * ROW2) + k * BSTEP * W, [[PIX, C], [1, XGRP * ROW2]])
                                       ).then_inc(s_xc[q % 3], 16)
                    pool.dma_start(xc[q % 3][24:32, :], grid[:, q * XGRP * ROW2:(q + 1) * XGRP * ROW2]
                                   ).then_inc(s_xc[q % 3], 16)



def layouts(x, L0_conv_W1, L0_conv_b1, L0_conv_W2, L0_conv_b2, L1_conv_fc0_w, L1_conv_fc0_b, L1_conv_w_w, L1_conv_w_b,
            L1_conv_sp_w1, L1_conv_sp_w2, L1_conv_betas, L1_conv_fc1_w, L1_conv_fc1_b, L1_conv_fc2_w, L1_conv_fc2_b):
    w1, w2, b1, b2 = (np.asarray(a) for a in (L0_conv_W1, L0_conv_W2, L0_conv_b1, L0_conv_b2))
    conv1_w = np.zeros((2, 8, C, 2, HID), np.float32)
    for tap in range(9):
        if tap != 4:
            for c in range(C):
                if c * 9 + tap < 9 * C - 1:
                    for half in range(2):
                        conv1_w[half, tap - (tap > 4), c, half] = w1[c * 9 + tap]
    conv2_w = np.zeros((4, HID, 4, C), np.float32)
    for n in range(4):
        conv2_w[n, :, n] = w2
    fc0, ww = np.asarray(L1_conv_fc0_w), np.asarray(L1_conv_w_w)
    lift_t = np.zeros((NBLK, G, WID, 128), np.float32)
    mix_w = np.zeros((NBLK, G, WID, LAYERS, NBLK, G, WID), np.float32)
    for k in range(NBLK):
        for g in range(G):
            for n in range(SC):
                lift_t[k, g, :, C * k + SC * g + n] = fc0[g, :, n]
            lift_t[k, g, :, C * NBLK + k] = fc0[g, :, SC]
            lift_t[k, g, :, C * NBLK + NBLK] = fc0[g, :, SC + 1]
            mix_w[k, g, :, :, k, g, :] = ww[:, g].transpose(2, 0, 1)
    lift_g = np.zeros((G, 32, SC + 3, WID), np.float32)
    lift_g[:, :, :SC + 2] = fc0.transpose(0, 2, 1)[:, None]
    lift_g[:, :, SC + 2] = np.asarray(L1_conv_fc0_b).reshape(G, 1, WID)
    spec = np.concatenate([np.asarray(L1_conv_sp_w1), np.asarray(L1_conv_sp_w2)], 4)
    spec_w = np.zeros((LAYERS, G, 32, WID * WID * 2 * KY), np.float32)
    spec_w[:, :, :KX] = spec.transpose(0, 1, 4, 2, 3, 5, 6).reshape(LAYERS, G, KX, -1)
    be = np.asarray(L1_conv_betas)
    betas = np.zeros((128, 12), np.float32)
    betas[:NBLK * CH, 0:4] = np.tile(np.repeat(be, WID, axis=1), (1, NBLK)).T
    betas[:, 4:8] = np.repeat(be, 32, axis=1).T
    betas[:, 8:12] = be[3][None]
    f1, f2 = np.asarray(L1_conv_fc1_w), np.asarray(L1_conv_fc2_w)
    fc1_w = np.zeros((3, G, WID, G, FF), np.float32)
    fc2_w = np.zeros((FF, G, 4, G, SC), np.float32)
    for g in range(G):
        fc1_w[:, g, :, g, :] = f1[g].T[None]
        fc2_w[:, g, 0, g, :] = f2[g].T
    fwd_row, fwd_col, inv_row, inv_col = fourier_tables()
    return {
        "x": np.asarray(x), "conv1_w": conv1_w.reshape(128, 64), "conv1_b": np.tile(b1, 4)[:, None],
        "conv2_w": conv2_w.reshape(128, 32), "conv2_b": np.tile(b2, 16)[:, None],
        "lift_t": lift_t.reshape(NBLK * CH, 128), "lift_g": lift_g.reshape(128, SC + 3, WID),
        "lift_b": np.tile(np.asarray(L1_conv_fc0_b), NBLK)[:, None],
        "mix_w": mix_w.reshape(NBLK * CH, LAYERS, NBLK * CH), "mix_b": np.tile(np.asarray(L1_conv_w_b), (1, NBLK)).T,
        "spec_w": spec_w.reshape(LAYERS, 128, -1), "betas": betas, "fc1_w": fc1_w.reshape(3 * CH, G * FF),
        "fc1_b": np.asarray(L1_conv_fc1_b).reshape(G, FF).T, "fc2_w": fc2_w.reshape(FF, G, 32),
        "fc2_b": np.tile(np.asarray(L1_conv_fc2_b), 16)[:, None], "fwd_row": fwd_row, "turn_id": turn_columns(),
        "fwd_col": fwd_col,
        "inv_row": inv_row, "inv_col": inv_col, "grid": grid_rows(), "gridf": grid_modes(),
        "gmean": group_mean(), "signs": split_signs(),
    }


def kernel(**inputs):
    import concourse.bacc as bacc
    from concourse.bass_utils import run_bass_kernel_spmd

    arrays = {f"in_{k}": np.ascontiguousarray(v) for k, v in layouts(**inputs).items()}
    nc = bacc.Bacc("TRN2", target_bir_lowering=False, num_devices=1)
    args = {k[3:]: nc.dram_tensor(k, a.shape, mybir.dt.from_np(a.dtype), kind="ExternalInput")
            for k, a in arrays.items()}
    nb = arrays["in_x"].shape[0]
    out = nc.dram_tensor("out_x", arrays["in_x"].shape, F32, kind="ExternalOutput")
    ins = {k: v if k in ("x",) else v.ap() for k, v in args.items()}
    program(nc, nb, out=out, **ins)
    r = run_bass_kernel_spmd(nc, [arrays], core_ids=[0])
    return r.results[0]["out_x"]
```
